# Optimizing a Trainium2 kernel written in Bass

```python
import numpy as np
import jax
import jax.numpy as jnp

def _softmax(x, axis=-1):
    return jax.nn.softmax(x, axis=axis)

def _gelu(x):
    return jax.nn.gelu(x, approximate=True)

def _silu(x):
    return jax.nn.silu(x)

def _sigmoid(x):
    return jax.nn.sigmoid(x)

def _layernorm(x, axis=-1, eps=1e-05):
    m = jnp.mean(x, axis=axis, keepdims=True)
    v = jnp.var(x, axis=axis, keepdims=True)
    return (x - m) / jnp.sqrt(v + eps)

def _scatter_add(tgt, idx, src, axis=0):
    return tgt.at[idx].add(src)

def _segment_sum(src, seg, n):
    return jax.ops.segment_sum(src, seg, n)
kernel_name = 'mk_macaron_d1_jaxref_r4_022d03'

def setup_inputs(seed: int=0):
    np.random.seed(seed)
    _w = jnp.asarray

    def _L0_attn_setup():
        import jax, jax.numpy as jnp
        import numpy as np
        B, S, E, H = (2, 512, 512, 16)
        HD = E // H
        EPS = 1e-05

        def _retention(x, Wq, bq, Wk, bk, Wv, bv, Wg, bg, Wo, bo, gn_w, gn_b, decay):
            b, s, e = x.shape
            h = decay.shape[0]
            hd = e // h
            scaling = hd ** (-0.5)

            def heads(t):
                return t.reshape(b, s, h, hd).transpose(0, 2, 1, 3)
            q = heads((x @ Wq + bq) * scaling)
            k = heads(x @ Wk + bk)
            v = heads(x @ Wv + bv)
            idx = jnp.arange(s)
            diff = idx[:, None] - idx[None, :]
            causal = diff >= 0
            diff_c = jnp.where(causal, diff, 0).astype(jnp.float32)
            D = jnp.where(causal[None], jnp.exp(decay[:, None, None] * diff_c[None]), 0.0)
            ret = jnp.einsum('bhid,bhjd->bhij', q, k) * D[None]
            scale = jnp.clip(jnp.abs(jax.lax.stop_gradient(ret).sum(-1, keepdims=True)), 1.0, None)
            ret = ret / scale
            attn = jnp.einsum('bhij,bhjd->bhid', ret, v)
            attn = attn.transpose(0, 2, 1, 3).reshape(b, s, e)
            g = attn.reshape(b, s, h, hd)
            mu = g.mean(-1, keepdims=True)
            var = g.var(-1, keepdims=True)
            g = (g - mu) / jnp.sqrt(var + EPS)
            g = g.reshape(b, s, e) * gn_w + gn_b
            gate = jax.nn.silu(x @ Wg + bg)
            return gate * g @ Wo + bo
        key = jax.random.key(seed)
        ks = jax.random.split(key, 12)
        std = 0.02

        def lin(k, din, dout):
            kw, kb = jax.random.split(k)
            W = jax.random.normal(kw, (din, dout), jnp.float32) * std
            b = jnp.zeros((dout,), jnp.float32)
            return (W, b)
        x = jax.random.normal(ks[0], (B, S, E), jnp.float32)
        Wq, bq = lin(ks[1], E, E)
        Wk, bk = lin(ks[2], E, E)
        Wv, bv = lin(ks[3], E, E)
        Wg, bg = lin(ks[4], E, E)
        Wo, bo = lin(ks[5], E, E)
        gn_w = jnp.ones((E,), jnp.float32)
        gn_b = jnp.zeros((E,), jnp.float32)
        decay = jnp.log(1.0 - 2.0 ** (-5.0 - jnp.arange(H, dtype=jnp.float32)))
        return dict(x=x, Wq=Wq, bq=bq, Wk=Wk, bk=bk, Wv=Wv, bv=bv, Wg=Wg, bg=bg, Wo=Wo, bo=bo, gn_w=gn_w, gn_b=gn_b, decay=decay)
    _L0_attn_in = _L0_attn_setup()

    def _L0_ffn_setup():
        import math
        import jax, jax.numpy as jnp
        import numpy as np
        NUM_EXPERTS = 8
        TOP_K = 2
        CAP_FACTOR = 1.25
        D_MODEL = 512
        D_HIDDEN = 2048
        B, S = (4, 512)
        key = jax.random.key(seed)
        ks = jax.random.split(key, 6)
        x = jax.random.normal(ks[0], (B, S, D_MODEL), dtype=jnp.float32)
        gating_w = jax.random.normal(ks[1], (D_MODEL, NUM_EXPERTS), dtype=jnp.float32) * (1.0 / math.sqrt(D_MODEL))
        w1 = jax.random.normal(ks[2], (NUM_EXPERTS, D_MODEL, D_HIDDEN), dtype=jnp.float32) * (1.0 / math.sqrt(D_MODEL))
        b1 = jnp.zeros((NUM_EXPERTS, D_HIDDEN), dtype=jnp.float32)
        w2 = jax.random.normal(ks[3], (NUM_EXPERTS, D_HIDDEN, D_MODEL), dtype=jnp.float32) * (1.0 / math.sqrt(D_HIDDEN))
        b2 = jnp.zeros((NUM_EXPERTS, D_MODEL), dtype=jnp.float32)
        return {'x': x, 'gating_w': gating_w, 'w1': w1, 'b1': b1, 'w2': w2, 'b2': b2}
    _L0_ffn_in = _L0_ffn_setup()
    _d = {'L0_attn_x': _L0_attn_in['x'], 'L0_attn_Wq': _L0_attn_in['Wq'], 'L0_attn_bq': _L0_attn_in['bq'], 'L0_attn_Wk': _L0_attn_in['Wk'], 'L0_attn_bk': _L0_attn_in['bk'], 'L0_attn_Wv': _L0_attn_in['Wv'], 'L0_attn_bv': _L0_attn_in['bv'], 'L0_attn_Wg': _L0_attn_in['Wg'], 'L0_attn_bg': _L0_attn_in['bg'], 'L0_attn_Wo': _L0_attn_in['Wo'], 'L0_attn_bo': _L0_attn_in['bo'], 'L0_attn_gn_w': _L0_attn_in['gn_w'], 'L0_attn_gn_b': _L0_attn_in['gn_b'], 'L0_attn_decay': _L0_attn_in['decay'], 'L0_ffn_gating_w': _L0_ffn_in['gating_w'], 'L0_ffn_w1': _L0_ffn_in['w1'], 'L0_ffn_b1': _L0_ffn_in['b1'], 'L0_ffn_w2': _L0_ffn_in['w2'], 'L0_ffn_b2': _L0_ffn_in['b2']}
    _x0 = _d['L0_attn_x']
    _d['L0_attn_x'] = jax.random.normal(jax.random.fold_in(jax.random.key(seed), 1), (4, 512, 512), dtype=_x0.dtype)
    del _x0
    return _d

def reference(L0_attn_x, L0_attn_Wq, L0_attn_bq, L0_attn_Wk, L0_attn_bk, L0_attn_Wv, L0_attn_bv, L0_attn_Wg, L0_attn_bg, L0_attn_Wo, L0_attn_bo, L0_attn_gn_w, L0_attn_gn_b, L0_attn_decay, L0_ffn_gating_w, L0_ffn_w1, L0_ffn_b1, L0_ffn_w2, L0_ffn_b2):

    def _L0_attn_ref(x, Wq, bq, Wk, bk, Wv, bv, Wg, bg, Wo, bo, gn_w, gn_b, decay):
        import jax, jax.numpy as jnp
        import numpy as np
        B, S, E, H = (2, 512, 512, 16)
        HD = E // H
        EPS = 1e-05

        def _retention(x, Wq, bq, Wk, bk, Wv, bv, Wg, bg, Wo, bo, gn_w, gn_b, decay):
            b, s, e = x.shape
            h = decay.shape[0]
            hd = e // h
            scaling = hd ** (-0.5)

            def heads(t):
                return t.reshape(b, s, h, hd).transpose(0, 2, 1, 3)
            q = heads((x @ Wq + bq) * scaling)
            k = heads(x @ Wk + bk)
            v = heads(x @ Wv + bv)
            idx = jnp.arange(s)
            diff = idx[:, None] - idx[None, :]
            causal = diff >= 0
            diff_c = jnp.where(causal, diff, 0).astype(jnp.float32)
            D = jnp.where(causal[None], jnp.exp(decay[:, None, None] * diff_c[None]), 0.0)
            ret = jnp.einsum('bhid,bhjd->bhij', q, k) * D[None]
            scale = jnp.clip(jnp.abs(jax.lax.stop_gradient(ret).sum(-1, keepdims=True)), 1.0, None)
            ret = ret / scale
            attn = jnp.einsum('bhij,bhjd->bhid', ret, v)
            attn = attn.transpose(0, 2, 1, 3).reshape(b, s, e)
            g = attn.reshape(b, s, h, hd)
            mu = g.mean(-1, keepdims=True)
            var = g.var(-1, keepdims=True)
            g = (g - mu) / jnp.sqrt(var + EPS)
            g = g.reshape(b, s, e) * gn_w + gn_b
            gate = jax.nn.silu(x @ Wg + bg)
            return gate * g @ Wo + bo
        return _retention(x, Wq, bq, Wk, bk, Wv, bv, Wg, bg, Wo, bo, gn_w, gn_b, decay)

    def _L0_ffn_ref(x, gating_w, w1, b1, w2, b2):
        import math
        import jax, jax.numpy as jnp
        import numpy as np
        NUM_EXPERTS = 8
        TOP_K = 2
        CAP_FACTOR = 1.25
        D_MODEL = 512
        D_HIDDEN = 2048
        B, S = (4, 512)
        b, s, d = x.shape
        x_flat = x.reshape(-1, d)
        T = x_flat.shape[0]
        num_items = T * TOP_K
        capacity = int(math.ceil(num_items / NUM_EXPERTS * CAP_FACTOR))
        gates = jax.nn.softmax(x_flat @ gating_w, axis=-1)
        topk_w, topk_idx = jax.lax.top_k(gates, TOP_K)
        norm_w = topk_w / (jnp.sum(topk_w, axis=-1, keepdims=True) + 1e-08)
        flat_e = topk_idx.reshape(-1)
        flat_t = jnp.repeat(jnp.arange(T, dtype=jnp.int32), TOP_K)
        flat_w = norm_w.reshape(-1)
        onehot = (flat_e[:, None] == jnp.arange(NUM_EXPERTS)[None, :]).astype(jnp.int32)
        pos_all = jnp.cumsum(onehot, axis=0) - 1
        position = jnp.take_along_axis(pos_all, flat_e[:, None].astype(jnp.int32), axis=1)[:, 0]
        valid = position < capacity
        pos_scatter = jnp.where(valid, position, capacity)
        buf = jnp.zeros((NUM_EXPERTS, capacity, d), dtype=x.dtype)
        buf = buf.at[flat_e, pos_scatter].set(x_flat[flat_t], mode='drop')
        h = jnp.maximum(jnp.einsum('ecd,edh->ech', buf, w1) + b1[:, None, :], 0.0)
        out_e = jnp.einsum('ech,ehd->ecd', h, w2) + b2[:, None, :]
        pos_gather = jnp.minimum(position, capacity - 1)
        gathered = out_e[flat_e, pos_gather]
        w_eff = jnp.where(valid, flat_w, 0.0)
        out_flat = jnp.zeros_like(x_flat).at[flat_t].add(gathered * w_eff[:, None])
        return out_flat.reshape(b, s, d)
    x = L0_attn_x
    x = x + 0.5 * _L0_ffn_ref(_layernorm(x, axis=-1), L0_ffn_gating_w, L0_ffn_w1, L0_ffn_b1, L0_ffn_w2, L0_ffn_b2)
    x = x + _L0_attn_ref(_layernorm(x, axis=-1), L0_attn_Wq, L0_attn_bq, L0_attn_Wk, L0_attn_bk, L0_attn_Wv, L0_attn_bv, L0_attn_Wg, L0_attn_bg, L0_attn_Wo, L0_attn_bo, L0_attn_gn_w, L0_attn_gn_b, L0_attn_decay)
    x = x + 0.5 * _L0_ffn_ref(_layernorm(x, axis=-1), L0_ffn_gating_w, L0_ffn_w1, L0_ffn_b1, L0_ffn_w2, L0_ffn_b2)
    return x

_drawn_inputs = setup_inputs


def setup_inputs(seed=0):
    import zlib

    import numpy as np

    out = dict(_drawn_inputs(seed))
    spreads = {'L0_attn_bq': (0.0, 0.1),
     'L0_attn_bk': (0.0, 0.1),
     'L0_attn_bv': (0.0, 0.1),
     'L0_attn_bg': (0.0, 0.1),
     'L0_attn_bo': (0.0, 0.1),
     'L0_attn_gn_w': (1.0, 0.2),
     'L0_attn_gn_b': (0.0, 0.402),
     'L0_ffn_b1': (0.0, 0.1),
     'L0_ffn_b2': (0.0, 0.1)}
    factors = {}
    for name, (base, spread) in spreads.items():
        noise = np.random.default_rng([zlib.crc32(name.encode()), seed]).standard_normal(out[name].shape)
        drawn = base * np.exp(spread * noise) if base else spread * noise
        out[name] = jnp.asarray(drawn.astype(out[name].dtype))
    for name, factor in factors.items():
        out[name] = (out[name] * factor).astype(out[name].dtype)
    return out
```

```python
from contextlib import ExitStack

import concourse.bass as bass
from concourse import mybir

ALU = mybir.AluOpType
ACT = mybir.ActivationFunctionType
AX_X = mybir.AxisListType.X
F32 = mybir.dt.float32
F32R = mybir.dt.float32r
BF16 = mybir.dt.bfloat16
U32 = mybir.dt.uint32

P = 128


class Steps:

    def __init__(self, eng, sem):
        self.eng, self.sem, self.base, self.n = eng, sem, 0, 0

    def loop(self, i, per):
        self.start, self.per, self.n = self.base + self.n, per, 0
        self.base = self.start + i * per

    def end(self, trips):
        assert self.n == self.per, (self.n, self.per)
        self.base, self.n = self.start + trips * self.per, 0

    def __call__(self, ins, wait=True):
        ins.then_inc(self.sem, 1)
        self.n += 1
        if wait:
            self.eng.wait_ge(self.sem, self.base + self.n)


def macaron_program(nc, x, Wq, bq, Wk, bk, Wv, bv, Wg, bg, Wo, bo, gn_w, gn_b, decay, gating_w, w1, b1, w2, b2, out):
    B, S, E = x.shape
    T = B * S
    NT = T // P
    KT = E // P
    NE, _, HID = w1.shape
    NG, GT = NT // 4, 4
    CAP = -(-(T * 2) * 5 // (NE * 4))
    ST = CAP // P
    HALF = CAP // 2
    HT = HID // P
    HPC = 2
    NC = HT // HPC
    CW = HPC * P
    RAW, SPL = 4, 2
    H = decay.shape[0]
    HD = E // H
    HPT = P // HD
    JT = S // P
    EPS = 1e-5
    FAR = 65536.0
    assert (NT, KT, ST, HALF, NE, HPT, JT, GT) == (16, 4, 5, 320, 8, 4, 4, 4)

    x_rows = x.rearrange("b s e -> (b s) e")
    out_rows = out.rearrange("b s e -> (b s) e")
    xbuf = nc.dram_tensor("xbuf", [(NE + 1) * CAP, E], F32).ap()
    obuf = nc.dram_tensor("obuf", [NE * CAP, E], F32).ap()
    x1_rows = nc.dram_tensor("x1", [T, E], F32).ap()
    x2_rows = nc.dram_tensor("x2", [T, E], F32).ap()

    with ExitStack() as ctx:
        def sb(name, shape, dt=F32, stack=ctx):
            return stack.enter_context(nc.sbuf_tensor(name, shape, dt))

        def sem(name):
            return ctx.enter_context(nc.semaphore(name))

        def sems(name, n):
            return [sem(f"{name}{i}") for i in range(n)]

        banks = [ctx.enter_context(nc.psum_tensor(f"bank{i}", [P, 512], F32)) for i in range(8)]
        out_bank, h_bank = banks[0:5], banks[5:8]

        ident = sb("ident", [P, P])
        upper = sb("upper", [P, P], BF16)
        ones_bf = sb("ones_bf", [P, P], BF16)
        ones32 = sb("ones32", [P, HD])
        headmean = sb("headmean", [P, P])
        iota8 = sb("iota8", [P, NE])
        slot0 = sb("slot0", [P, GT, NE])
        b1T = sb("b1T", [P, NE * HT])
        gw = sb("gw", [P, KT, NE])
        b1e = sb("b1e", [P, HT])
        epsc = sb("epsc", [P, 1])
        cols = sb("cols", [P, 6, KT])
        mv = sb("mv", [P, GT, 2])
        st6 = sb("st6", [P, GT, 6])
        var = sb("var", [P, GT])
        rstd = sb("rstd", [P, GT])
        newton = sb("newton", [P, GT])
        lg = sb("lg", [P, GT, NE])
        mx = sb("mx", [P, GT])
        ex = sb("ex", [P, GT, NE])
        sm = sb("sm", [P, GT])
        gates = sb("gates", [P, GT, NE])
        top = sb("top", [P, GT, 8])
        topi = sb("topi", [P, GT, 8], U32)
        topf = sb("topf", [P, GT, 2])
        oh = sb("oh", [P, GT, 2, NE])
        ohs = sb("ohs", [P, GT, NE], BF16)
        carry = sb("carry", [P, NE])
        count = sb("count", [P, GT, NE])
        gslot = sb("gslot", [P, GT, NE])
        sslot = sb("sslot", [P, GT, NE])
        pick = sb("pick", [P, GT, 2, NE])
        scf = sb("scf", [P, GT, 2])
        gaf = sb("gaf", [P, GT, 2])
        sci = sb("sci", [P, GT, 2], U32)
        tsum = sb("tsum", [P, GT])
        wk2 = sb("wk2", [P, GT, 2])
        vld = sb("vld", [P, GT, 2])
        gidx = sb("gidx", [P, NT, 2], U32)
        wgt = sb("wgt", [P, NT, 2])
        cidx = sb("cidx", [P, GT, 2], U32)
        xt = sb("xt", [P, GT, E])
        xn = sb("xn", [P, GT, E])
        xT = sb("xT", [P, GT, KT, P])
        ga = sb("ga", [P, GT, 2, E])
        b1rows, colrows = xT[:, 0, 0, :], xT[0:5 * KT, 1, 0, :]

        with ExitStack() as ffn:
            w1raw = sb("w1raw", [P, RAW, KT, CW], F32, ffn)
            w2raw = sb("w2raw", [P, RAW, HPC, E], F32, ffn)
            w1h = sb("w1h", [P, SPL, KT, CW], F32R, ffn)
            w1l = sb("w1l", [P, SPL, KT, CW], F32R, ffn)
            w2h = sb("w2h", [P, SPL, HPC, E], F32R, ffn)
            w2l = sb("w2l", [P, SPL, HPC, E], F32R, ffn)
            bTh = sb("bTh", [P, KT, CAP], F32R, ffn)
            bTl = sb("bTl", [P, KT, CAP], F32R, ffn)
            xg = sb("xg", [P, ST, E], F32, ffn)
            hf = sb("hf", [P, 2, CAP], F32, ffn)
            hh = sb("hh", [P, 4, CAP], F32R, ffn)
            hl = sb("hl", [P, 4, CAP], F32R, ffn)
            o = sb("o", [P, ST, E], F32, ffn)
            b2t = sb("b2t", [P, E], F32, ffn)
        with ExitStack() as att:
            wh = sb("wh", [P, 5, KT, E], F32R, att)
            wl = sb("wl", [P, 5, KT, E], F32R, att)
            xTh = sb("xTh", [P, KT, S], F32R, att)
            xTl = sb("xTl", [P, KT, S], F32R, att)
            qf = sb("qf", [P, S], F32, att)
            qh = sb("qh", [P, S], F32R, att)
            ql = sb("ql", [P, S], F32R, att)
            kf = sb("kf", [P, S], F32, att)
            kzh = sb("kzh", [P, HPT, S], F32R, att)
            kzl = sb("kzl", [P, HPT, S], F32R, att)
            v = sb("v", [P, JT, E], F32, att)
            dcy = sb("dcy", [P, HPT, S], F32, att)
            dif = sb("dif", [P, S], F32, att)
            gate = sb("gate", [P, 2, S], F32, att)
            gth = sb("gth", [P, KT, S], F32R, att)
            gtl = sb("gtl", [P, KT, S], F32R, att)
            bvt = sb("bvt", [P, E], F32, att)
            bot = sb("bot", [P, E], F32, att)
            dect = sb("dect", [P, H], F32, att)
        cen, egt, root = xn[:, 0], xn[:, 1], xn[:, 2]
        tmp = [xT[:, i, :, :].rearrange("p k t -> p (k t)") for i in range(GT)]
        sc = [ga[:, i // 2, i % 2, :] for i in range(2 * GT)]
        wst = [ga[:, 2 * i:2 * i + 2, :, :].rearrange("p a b e -> p (a b) e") for i in range(2)]

        const_ready = sem("const_ready")
        pool_step = sem("pool_step")
        dve_step = sem("dve_step")
        zero_ready = sem("zero_ready")
        zero_filled = sem("zero_filled")
        small_in = sem("small_in")
        biases_turned, biases_ready, b1e_ready = sem("biases_turned"), sem("biases_ready"), sem("b1e_ready")
        x_in = sems("x_in", GT)
        var_ready, ln_ready, rstd_ready = sem("var_ready"), sem("ln_ready"), sem("rstd_ready")
        xn_ready = sems("xn_ready", GT)
        xT_full = sem("xT_full")
        xT_copied = sems("xT_copied", GT)
        logits_full = sem("logits_full")
        logits_copied = sem("logits_copied")
        shifted = sem("shifted")
        exp_ready = sem("exp_ready")
        chosen = sem("chosen")
        counted = sem("counted")
        slots_ready = sem("slots_ready")
        scattered = sems("scattered", GT)
        w1_in, w2_in = sems("w1_in", RAW), sems("w2_in", RAW)
        w1_hi, w2_hi = sem("w1_hi"), sem("w2_hi")
        w1_split, w2_split = sems("w1_split", RAW), sems("w2_split", RAW)
        xg_in, b2_in = sem("xg_in"), sem("b2_in")
        turned, turned_hi, turned_split = sem("turned"), sem("turned_hi"), sem("turned_split")
        h_full, h_evac, h_hi, h_split = sem("h_full"), sem("h_evac"), sem("h_hi"), sem("h_split")
        b_done, o_ready = sem("b_done"), sem("o_ready")
        o_stored = sems("o_stored", ST)
        cidx_ready = sem("cidx_ready")
        gathered = sems("gathered", GT)
        residual_in = sems("residual_in", GT)
        y_ready = sems("y_ready", GT)
        y_stored = sems("y_stored", GT)
        aw_in = sems("aw_in", 2)
        aw_hi, aw_split = sem("aw_hi"), sem("aw_split")
        small2_in = sem("small2_in")
        negbg_ready, kz_zeroed, dif_ready = sem("negbg_ready"), sem("kz_zeroed"), sem("dif_ready")
        ax_in = sems("ax_in", GT)
        axn_ready = sem("axn_ready")
        aT_full, aT_hi, aT_split = sem("aT_full"), sem("aT_hi"), sem("aT_split")
        v_full, v_ready = sem("v_full"), sem("v_ready")
        q_full, q_evac, q_hi, q_split = sem("q_full"), sem("q_evac"), sem("q_hi"), sem("q_split")
        k_full, k_evac, k_hi, k_split = sem("k_full"), sem("k_evac"), sem("k_hi"), sem("k_split")
        g_full, g_exp, g_evac = sem("g_full"), sem("g_exp"), sem("g_evac")
        d_exp, d_ready = sem("d_exp"), sem("d_ready")
        s_full = sem("s_full")
        p_ready = sems("p_ready", HPT)
        pv_done = sem("pv_done")
        a_ready = sem("a_ready")
        mean_full, centred, squared = sem("mean_full"), sem("centred"), sem("squared")
        abs_ready, root_ready, eps_ready = sem("abs_ready"), sem("root_ready"), sem("eps_ready")
        var_full, var_read = sem("var_full"), sem("var_read")
        gt_ready, gt_hi, gt_split = sem("gt_ready"), sem("gt_hi"), sem("gt_split")
        o_full, x2_ready = sem("o_full"), sem("x2_ready")
        x2_stored = sems("x2_stored", GT)

        waits_carried = sem("waits_carried")

        def carry_wait(eng):
            eng.sem_inc(waits_carried, 1)

        block = ctx.enter_context(nc.Block())
        AG = NG

        order = [("t", i) for i in range(GT)] + [("v", i) for i in range(JT)] + [(n, 0) for n in "qkg"]
        for et in range(KT):
            if et + 1 < KT:
                order += [("q", et + 1), ("mean", et), ("k", et + 1), ("g", et + 1), ("var", et)]
            else:
                order += [("mean", et), ("var", et)]
        order += [("o", i) for i in range(GT)]
        pb = {user: n for n, user in enumerate(order)}
        assert len(order) % 2 == 0

        @block.sync
        def _(sp):
            sp.dma_start(gw[:], gating_w.rearrange("(k p) e -> p k e", p=P)).then_inc(small_in, 16)
            sp.dma_start(b1rows, b1.rearrange("e (t p) -> (e t) p", p=P)).then_inc(small_in, 16)
            for n, src in enumerate((bq, bk, bg, gn_w, gn_b)):
                sp.dma_start(colrows[n * KT:(n + 1) * KT, :], src.rearrange("(k p) -> k p", p=P)).then_inc(small_in, 16)

            def route_loads(f, src):
                if f:
                    for i in range(GT):
                        sp.wait_ge(x2_stored[i], 16 * AG)
                with sp.Fori(0, NG) as g:
                    for i in range(GT):
                        sp.wait_ge(xn_ready[i], f * NG + g)
                        sp.dma_start(xt[:, i, :], src[bass.ds((g * GT + i) * P, P), :]).then_inc(x_in[i], 16)

            def expert_loads(f):
                with sp.Fori(0, NE) as e:
                    ee = e + f * NE
                    for c in range(NC):
                        r, uses = c % RAW, ee * (NC // RAW) + c // RAW
                        sp.wait_ge(w1_split[r], uses)
                        sp.dma_start(w1raw[:, r], w1[bass.ds(e, 1), :, c * CW:(c + 1) * CW].rearrange(
                            "o (k p) n -> p (o k) n", p=P)).then_inc(w1_in[r], 16)
                        sp.wait_ge(w2_split[r], uses)
                        sp.dma_start(w2raw[:, r], w2[bass.ds(e, 1), c * CW:(c + 1) * CW, :].rearrange(
                            "o (t p) n -> p (o t) n", p=P)).then_inc(w2_in[r], 16)

            def combine_moves(f, src, dst):
                with sp.Fori(0, NG) as g:
                    k = g + f * NG
                    for i in range(GT):
                        sp.wait_ge(y_stored[i], 16 * k)
                        sp.dma_start(xt[:, i, :], src[bass.ds((g * GT + i) * P, P), :]).then_inc(residual_in[i], 16)
                    for i in range(GT):
                        sp.wait_ge(y_ready[i], k + 1)
                        sp.dma_start(dst[bass.ds((g * GT + i) * P, P), :], xt[:, i, :]).then_inc(y_stored[i], 16)

            def retention_moves():
                for i in range(GT):
                    sp.wait_ge(y_stored[i], 16 * NG)
                for t, src in ((bvt, bv), (bot, bo), (dect, decay)):
                    sp.dma_start(t[:], src.rearrange("(a n) -> a n", a=1).broadcast_to(t.shape)).then_inc(small2_in, 16)
                for n, w in enumerate((Wq, Wk, Wv, Wg, Wo)):
                    if n >= 2:
                        sp.wait_ge(aw_split, n - 1)
                    sp.dma_start(wst[n % 2], w.rearrange("(k p) n -> p k n", p=P)).then_inc(aw_in[n % 2], 16)
                with sp.Fori(0, AG) as b:
                    for i in range(GT):
                        sp.wait_ge(x2_stored[i], 16 * b)
                        sp.dma_start(xt[:, i, :], x1_rows[bass.ds((b * GT + i) * P, P), :]).then_inc(ax_in[i], 16)
                    for i in range(GT):
                        sp.wait_ge(x2_ready, b * GT + i + 1)
                        sp.dma_start(x2_rows[bass.ds((b * GT + i) * P, P), :], xt[:, i, :]).then_inc(x2_stored[i], 16)

            route_loads(0, x_rows)
            expert_loads(0)
            combine_moves(0, x_rows, x1_rows)
            retention_moves()
            route_loads(1, x2_rows)
            expert_loads(1)
            combine_moves(1, x2_rows, out_rows)
            for i in range(GT):
                sp.wait_ge(y_stored[i], 16 * 2 * NG)

        @block.gpsimd
        def _(pool):
            step = Steps(pool, pool_step)
            pool.memset(ga[:, 0, 0, :], 0.0).then_inc(zero_ready, 1)
            step(pool.memset(ident[:], 0.0), wait=False)
            step(pool.memset(upper[:], 1.0), wait=False)
            step(pool.memset(headmean[:], 1.0 / HD), wait=False)
            step(pool.iota(iota8[:], [[1, NE]], base=0, channel_multiplier=0,
                           allow_small_or_imprecise_dtypes=True), wait=False)
            step(pool.iota(slot0[:], [[0, GT], [CAP, NE]], base=0, channel_multiplier=0,
                           allow_small_or_imprecise_dtypes=True))
            pool.affine_select(out=ident[:], in_=ident[:], compare_op=ALU.not_equal, fill=1.0,
                               base=0, pattern=[[-1, P]], channel_multiplier=1).then_inc(const_ready, 1)
            pool.affine_select(out=upper[:], in_=upper[:], compare_op=ALU.is_gt, fill=0.0,
                               base=0, pattern=[[1, P]], channel_multiplier=-1).then_inc(const_ready, 1)
            hm = headmean[:].rearrange("p (h d) -> p h d", d=HD)
            step(pool.affine_select(out=hm, in_=hm, compare_op=ALU.is_ge, fill=0.0,
                                    base=0, pattern=[[-HD, HPT], [0, HD]], channel_multiplier=1))
            pool.affine_select(out=hm, in_=hm, compare_op=ALU.is_ge, fill=0.0,
                               base=HD - 1, pattern=[[HD, HPT], [0, HD]], channel_multiplier=-1).then_inc(const_ready, 1)
            pool.memset(ones_bf[:], 1.0).then_inc(const_ready, 1)
            pool.memset(ones32[:], 1.0).then_inc(const_ready, 1)
            pool.memset(epsc[:], EPS).then_inc(eps_ready, 1)
            pool.memset(carry[:], 0.0).then_inc(const_ready, 1)

            bound = pool.to_reg(NE * CAP - 1)
            zero = pool.to_reg(0.0)

            def scatter(f):
                if f == 0:
                    pool.wait_ge(zero_filled, 16 * 3)
                with pool.Fori(0, NG) as g:
                    pool.wait_ge(slots_ready, f * NG + g + 1)
                    carry_wait(pool)
                    for i in range(GT):
                        for c in range(2):
                            pool.indirect_dma_start(
                                out=xbuf, out_offset=bass.IndirectOffsetOnAxis(ap=sci[:, i, c:c + 1], axis=0),
                                in_=xn[:, i, :], in_offset=None, bounds_check=bound,
                                oob_is_err=False).then_inc(scattered[i], 16)

            def load_expert_rows(e, used):
                pool.wait_ge(turned, used)
                pool.dma_start(xg[:], xbuf[bass.ds(e * CAP, CAP), :].rearrange(
                    "(s p) d -> p s d", p=P)).then_inc(xg_in, 16)

            def expert_moves(f):
                for i in range(GT):
                    pool.wait_ge(scattered[i], 32 * NG * (f + 1))
                load_expert_rows(0, f * ST * (NE + 1))
                with pool.Fori(0, NE) as e:
                    ee = e + f * NE
                    pool.wait_ge(o_ready, ee * ST)
                    pool.dma_start(b2t[:], b2[bass.ds(e, 1), :].broadcast_to([P, E])).then_inc(b2_in, 16)
                    load_expert_rows(e + 1, e * ST + (f * ST * (NE + 1) + ST))
                    for s in range(ST):
                        pool.wait_ge(o_ready, ee * ST + s + 1)
                        pool.dma_start(obuf[bass.ds(e * CAP + s * P, P), :], o[:, s, :]).then_inc(o_stored[s], 16)

            def gather(f):
                for s in range(ST):
                    pool.wait_ge(o_stored[s], 16 * NE * (f + 1))
                with pool.Fori(0, NG) as g:
                    k = g + f * NG
                    for i in range(GT):
                        pool.wait_ge(y_ready[i], k)
                    pool.tensor_copy(cidx[:], gidx[:, bass.ds(g * GT, GT), :]).then_inc(cidx_ready, 1)
                    pool.wait_ge(cidx_ready, k + 1)
                    carry_wait(pool)
                    for i in range(GT):
                        for c in range(2):
                            pool.indirect_dma_start(
                                out=ga[:, i, c, :], out_offset=None, in_=obuf,
                                in_offset=bass.IndirectOffsetOnAxis(ap=cidx[:, i, c:c + 1], axis=0),
                                bounds_check=bound, oob_is_err=False).then_inc(gathered[i], 16)

            def masks():
                for i in range(GT):
                    pool.wait_ge(y_stored[i], 16 * NG)
                pool.memset(kzh[:].bitcast(U32), 0).then_inc(kz_zeroed, 1)
                pool.memset(kzl[:].bitcast(U32), 0).then_inc(kz_zeroed, 1)
                step(pool.iota(dif[:], [[1, S]], base=0, channel_multiplier=-1,
                               allow_small_or_imprecise_dtypes=True))
                pool.tensor_scalar(dif[:], dif[:], 0.0, None, ALU.max).then_inc(dif_ready, 1)
                with pool.Fori(0, AG) as b:
                    for et in range(KT):
                        pool.wait_ge(d_exp, b * KT + et + 1)
                        carry_wait(pool)
                        for h in range(HPT):
                            m = pool.affine_select(out=dcy[:, h, 0:P], in_=dcy[:, h, 0:P], compare_op=ALU.is_ge,
                                                   fill=zero, base=0, pattern=[[1, P]], channel_multiplier=-1)
                        m.then_inc(d_ready, 1)

            scatter(0)
            expert_moves(0)
            gather(0)
            masks()
            scatter(1)
            expert_moves(1)
            gather(1)

        @block.scalar
        def _(act):
            act.preload_act_table_set("natural_log_exp_and_others")
            act.wait_ge(zero_ready, 1)
            rows = (NE + 1) * CAP // 3
            for n in range(3):
                act.dma_start(xbuf[n * rows:(n + 1) * rows, :].rearrange("(t p) d -> p t d", p=P),
                              ga[:, 0, 0:1, :].broadcast_to([P, rows // P, E])).then_inc(zero_filled, 16)

            def inverse_root(groups):
                act.wait_ge(var_ready, groups + 1)
                act.activation(rstd[:], var[:], ACT.Ln).then_inc(ln_ready, 1)
                act.wait_ge(ln_ready, groups + 1)
                act.activation(rstd[:], rstd[:], ACT.Exp, scale=-0.5).then_inc(rstd_ready, 1)

            def route(f):
                with act.Fori(0, NG) as g:
                    k = g + f * NG
                    inverse_root(k + f * AG)
                    act.wait_ge(logits_full, k * GT)
                    for i in range(GT):
                        act.wait_ge(xT_full, k * GT + (i + 1))
                        act.activation(xT[:, i].rearrange("p k t -> p (k t)"), h_bank[i % 2][:], ACT.Copy).then_inc(xT_copied[i], 1)
                    act.wait_ge(shifted, k + 1)
                    act.activation(ex[:], lg[:], ACT.Exp).then_inc(exp_ready, 1)

            def turn_evac(base):
                for s in range(ST):
                    act.wait_ge(turned, base + (s + 1))
                    act.activation(bTh[:, :, s * P:(s + 1) * P], h_bank[(s + 2) % 3][:].rearrange("p (k t) -> p k t", k=KT),
                                   ACT.Copy).then_inc(turned_hi, 1)

            def experts(f):
                def body(e, first_weights=False, last=False):
                    ee = e + f * NE

                    def split_w1(c):
                        act.wait_ge(w1_in[c % RAW], 16 * (c // RAW + 1) + ee * (16 * NC // RAW))
                        act.wait_ge(h_full, ee * (2 * HT) + max((c - SPL + 1) * 2 * HPC, 0))
                        act.activation(w1h[:, c % SPL], w1raw[:, c % RAW], ACT.Copy).then_inc(w1_hi, 1)

                    def split_w2(c):
                        act.wait_ge(w2_in[c % RAW], 16 * (c // RAW + 1) + ee * (16 * NC // RAW))
                        act.wait_ge(b_done, ee * HT + max((c - SPL + 1) * HPC, 0))
                        act.activation(w2h[:, c % SPL], w2raw[:, c % RAW], ACT.Copy).then_inc(w2_hi, 1)

                    if first_weights:
                        split_w1(0)
                        split_w1(1)
                        split_w2(0)
                        return
                    act.activation(b1e[:], b1T[:, bass.ds(e * HT, HT)], ACT.Copy).then_inc(b1e_ready, 1)
                    act.wait_ge(b1e_ready, ee + 1)
                    for n in range(HT):
                        if n in (0, 1):
                            act.wait_ge(h_split, ee * HT)
                        else:
                            act.wait_ge(h_split, ee * HT + (n - 1))
                        for half in range(2):
                            act.wait_ge(h_full, ee * (2 * HT) + (2 * n + half + 1))
                            act.activation(hf[:, n % 2, half * HALF:(half + 1) * HALF], h_bank[(2 * n + half) % 3][:, 0:HALF],
                                           ACT.Relu, bias=b1e[:, n:n + 1]).then_inc(h_evac, 1)
                        act.wait_ge(h_evac, ee * (2 * HT) + (2 * n + 2))
                        act.wait_ge(b_done, ee * HT + max(n - 3, 0))
                        act.activation(hh[:, n % 4], hf[:, n % 2], ACT.Copy).then_inc(h_hi, 1)
                        if n % 2 == 1:
                            c = n // 2
                            if c + 2 < NC or not last:
                                split_w1(c + 2)
                            if c + 1 < NC or not last:
                                split_w2(c + 1)
                    turn_evac(ee * ST + (f * ST + ST))

                body(0, first_weights=True)
                turn_evac(f * ST * (NE + 1))
                with act.Fori(0, NE - 1) as e:
                    body(e)
                body(NE - 1, last=True)

            def retention():
                for i in range(GT):
                    act.wait_ge(y_stored[i], 16 * NG)
                for n in range(5):
                    act.wait_ge(aw_in[n % 2], 16 * (n // 2 + 1))
                    act.activation(wh[:, n], wst[n % 2], ACT.Copy).then_inc(aw_hi, 1)
                act.wait_ge(small2_in, 16 * 3)
                act.mul(cols[:, 5], cols[:, 2], -1.0).then_inc(negbg_ready, 1)
                act.wait_ge(negbg_ready, 1)
                act.wait_ge(kz_zeroed, 2)
                act.wait_ge(dif_ready, 1)
                with act.Fori(0, AG) as b:
                    m = b * KT

                    def query(et):
                        act.wait_ge(q_evac, m + (et + 1))
                        act.activation(qh[:], qf[:], ACT.Copy).then_inc(q_hi, 1)

                    def key_gate_decay(et):
                        act.wait_ge(k_full, m + (et + 1))
                        act.wait_ge(k_split, m + et)
                        act.activation(kf[:], banks[pb[("k", et)] % 2][:], ACT.Identity, bias=cols[:, 1, et:et + 1]).then_inc(k_evac, 1)
                        act.wait_ge(k_evac, m + (et + 1))
                        for h in range(HPT):
                            r = slice(h * HD, (h + 1) * HD)
                            ins = act.activation(kzh[r, h], kf[r, :], ACT.Copy)
                        ins.then_inc(k_hi, 1)
                        act.wait_ge(g_full, m + (et + 1))
                        act.activation(egt[:], banks[pb[("g", et)] % 2][:], ACT.Exp, scale=-1.0, bias=cols[:, 5, et:et + 1]).then_inc(g_exp, 1)
                        for h in range(HPT):
                            act.wait_ge(p_ready[h], (m + et) * JT)
                        for h in range(HPT):
                            hd = et * HPT + h
                            ins = act.activation(dcy[:, h], dif[:], ACT.Exp, scale=dect[:, hd:hd + 1])
                        ins.then_inc(d_exp, 1)

                    inverse_root(b + NG)
                    for i in range(GT):
                        act.wait_ge(aT_full, b * GT + (i + 1))
                        act.activation(xTh[:, :, i * P:(i + 1) * P], banks[pb[("t", i)] % 2][:].rearrange("p (k t) -> p k t", k=KT),
                                       ACT.Copy).then_inc(aT_hi, 1)
                    query(0)
                    key_gate_decay(0)
                    for et in range(KT):
                        act.wait_ge(pv_done, (b * KT + et) * JT + JT)
                        act.activation(tmp[0], banks[7][:], ACT.Abs).then_inc(abs_ready, 1)
                        if et + 1 < KT:
                            query(et + 1)
                        act.wait_ge(centred, b * KT + (et + 1))
                        act.activation(tmp[2], cen[:], ACT.Square).then_inc(squared, 1)
                        if et + 1 < KT:
                            key_gate_decay(et + 1)
                        act.wait_ge(var_full, b * KT + (et + 1))
                        act.wait_ge(eps_ready, 1)
                        act.activation(root, banks[pb[("var", et)] % 2][:], ACT.Ln, bias=epsc[:]).then_inc(var_read, 1)
                        act.wait_ge(var_read, b * KT + (et + 1))
                        act.activation(root, root, ACT.Exp, scale=-0.5).then_inc(root_ready, 1)
                        act.wait_ge(gt_ready, b * KT + (et + 1))
                        act.activation(gth[:, et], tmp[3], ACT.Copy).then_inc(gt_hi, 1)

            route(0)
            experts(0)
            retention()
            route(1)
            experts(1)

        @block.vector
        def _(dve):
            step = Steps(dve, dve_step)
            dve.wait_ge(biases_turned, 2)
            dve.tensor_copy(cols[:, 0:5].rearrange("p n k -> p (n k)"), out_bank[3][:, 0:5 * KT]).then_inc(biases_ready, 1)
            dve.tensor_copy(b1T[:], out_bank[2][:, 0:NE * HT]).then_inc(biases_ready, 1)
            dve.wait_ge(const_ready, 6)

            def normalise(loaded, ready, free, groups):
                for i in range(GT):
                    dve.wait_ge(loaded[i][0], loaded[i][1])
                    ins = dve.bn_stats(st6[:, i], xt[:, i])
                step(ins)
                carry_wait(dve)
                for i in range(GT):
                    ins = dve.bn_aggr(mv[:, i], st6[:, i])
                step(ins)
                dve.tensor_scalar(var[:], mv[:, :, 1], EPS, None, ALU.add).then_inc(var_ready, 1)
                dve.wait_ge(rstd_ready, groups + 1)
                step(dve.tensor_tensor(newton[:], rstd[:], rstd[:], ALU.mult))
                step(dve.tensor_tensor(newton[:], newton[:], var[:], ALU.mult))
                step(dve.tensor_scalar(newton[:], newton[:], -0.5, 1.5, ALU.mult, ALU.add))
                step(dve.tensor_tensor(rstd[:], rstd[:], newton[:], ALU.mult))
                for i in range(GT):
                    if free:
                        dve.wait_ge(free[i][0], free[i][1])
                    dve.tensor_scalar(xn[:, i], xt[:, i], mv[:, i, 0:1], rstd[:, i:i + 1],
                                      ALU.subtract, ALU.mult).then_inc(ready[i], 1)

            def route(f):
                if f:
                    step(dve.memset(carry[:], 0.0))
                with dve.Fori(0, NG) as g:
                    k = g + f * NG
                    step.loop(g, 29)
                    normalise([(x_in[i], k * 16 + 16) for i in range(GT)], xn_ready,
                              [(scattered[i], k * 32) for i in range(GT)], k + f * AG)
                    dve.wait_ge(logits_full, k * GT + GT)
                    dve.tensor_copy(lg[:].rearrange("p g e -> p (g e)"), out_bank[0][:, 0:GT * NE]).then_inc(logits_copied, 1)
                    dve.wait_ge(logits_copied, k + 1)
                    step(dve.tensor_reduce(mx[:], lg[:], AX_X, ALU.max))
                    dve.tensor_tensor(lg[:], lg[:], mx[:].unsqueeze(2).broadcast_to([P, GT, NE]), ALU.subtract).then_inc(shifted, 1)
                    dve.wait_ge(exp_ready, k + 1)
                    step(dve.tensor_reduce(sm[:], ex[:], AX_X, ALU.add))
                    step(dve.reciprocal(sm[:], sm[:]))
                    ins = (dve.tensor_tensor(gates[:], ex[:], sm[:].unsqueeze(2).broadcast_to([P, GT, NE]), ALU.mult))
                    step(ins)
                    carry_wait(dve)
                    for i in range(GT):
                        ins = dve.max(top[:, i], gates[:, i])
                    step(ins)
                    carry_wait(dve)
                    for i in range(GT):
                        ins = dve.max_index(topi[:, i], top[:, i], gates[:, i])
                    step(ins)
                    step(dve.tensor_copy(topf[:], topi[:, :, 0:2]))
                    step(dve.tensor_tensor(oh[:], iota8[:].unsqueeze(1).unsqueeze(1).broadcast_to([P, GT, 2, NE]),
                                           topf[:].unsqueeze(3).broadcast_to([P, GT, 2, NE]), ALU.is_equal))
                    dve.tensor_tensor(ohs[:], oh[:, :, 0], oh[:, :, 1], ALU.add).then_inc(chosen, 1)
                    step(dve.scalar_tensor_tensor(tsum[:], top[:, :, 0], 1e-8, top[:, :, 1], ALU.add, ALU.add))
                    step(dve.reciprocal(tsum[:], tsum[:]))
                    step(dve.tensor_tensor(wk2[:], top[:, :, 0:2], tsum[:].unsqueeze(2).broadcast_to([P, GT, 2]), ALU.mult))
                    dve.wait_ge(counted, k + 1)
                    step(dve.tensor_tensor(count[:], out_bank[1][:, 0:GT * NE].rearrange("p (g e) -> p g e", g=GT),
                                           carry[:].unsqueeze(1).broadcast_to([P, GT, NE]), ALU.add))
                    step(dve.tensor_tensor(carry[:], carry[:], out_bank[1][:, GT * NE:(GT + 1) * NE], ALU.add), wait=False)
                    step(dve.scalar_tensor_tensor(gslot[:], count[:], float(CAP - 1), slot0[:], ALU.min, ALU.add), wait=False)
                    step(dve.tensor_scalar(sslot[:], count[:], float(CAP), FAR, ALU.is_ge, ALU.mult))
                    step(dve.tensor_tensor(sslot[:], sslot[:], gslot[:], ALU.add))
                    step(dve.tensor_tensor(pick[:], oh[:], sslot[:].unsqueeze(2).broadcast_to([P, GT, 2, NE]), ALU.mult))
                    step(dve.tensor_reduce(scf[:], pick[:], AX_X, ALU.add))
                    dve.tensor_copy(sci[:], scf[:]).then_inc(slots_ready, 1)
                    step(dve.tensor_tensor(pick[:], oh[:], gslot[:].unsqueeze(2).broadcast_to([P, GT, 2, NE]), ALU.mult))
                    step(dve.tensor_reduce(gaf[:], pick[:], AX_X, ALU.add))
                    step(dve.tensor_copy(gidx[:, bass.ds(g * GT, GT), :], gaf[:]), wait=False)
                    step(dve.tensor_scalar(vld[:], scf[:], FAR, 0.5, ALU.is_lt, ALU.mult))
                    step(dve.tensor_tensor(wgt[:, bass.ds(g * GT, GT), :], wk2[:], vld[:], ALU.mult))
                step.end(NG)

            def turn_split(base):
                for s in range(ST):
                    dve.wait_ge(turned_hi, base + (s + 1))
                    dve.tensor_tensor(bTl[:, :, s * P:(s + 1) * P], h_bank[(s + 2) % 3][:].rearrange("p (k t) -> p k t", k=KT),
                                      bTh[:, :, s * P:(s + 1) * P].bitcast(F32), ALU.subtract).then_inc(turned_split, 1)

            def experts(f):
                def body(e, first_weights=False, last=False):
                    ee = e + f * NE

                    def split_w1(c):
                        dve.wait_ge(w1_hi, ee * NC + (c + 1))
                        dve.tensor_tensor(w1l[:, c % SPL], w1raw[:, c % RAW], w1h[:, c % SPL].bitcast(F32),
                                          ALU.subtract).then_inc(w1_split[c % RAW], 1)

                    def split_w2(c):
                        dve.wait_ge(w2_hi, ee * NC + (c + 1))
                        dve.tensor_tensor(w2l[:, c % SPL], w2raw[:, c % RAW], w2h[:, c % SPL].bitcast(F32),
                                          ALU.subtract).then_inc(w2_split[c % RAW], 1)

                    if first_weights:
                        split_w1(0)
                        split_w1(1)
                        split_w2(0)
                        return
                    for n in range(HT):
                        dve.wait_ge(h_hi, ee * HT + (n + 1))
                        dve.tensor_tensor(hl[:, n % 4], hf[:, n % 2], hh[:, n % 4].bitcast(F32), ALU.subtract).then_inc(h_split, 1)
                        if n % 2 == 1:
                            c = n // 2
                            if c + 2 < NC or not last:
                                split_w1(c + 2)
                            if c + 1 < NC or not last:
                                split_w2(c + 1)
                    turn_split(ee * ST + (f * ST + ST))
                    dve.wait_ge(b_done, ee * HT + HT)
                    dve.wait_ge(b2_in, ee * 16 + 16)
                    for s in range(ST):
                        dve.wait_ge(o_stored[s], ee * 16)
                        dve.tensor_tensor(o[:, s], out_bank[s][:], b2t[:], ALU.add).then_inc(o_ready, 1)

                body(0, first_weights=True)
                turn_split(f * ST * (NE + 1))
                with dve.Fori(0, NE - 1) as e:
                    body(e)
                body(NE - 1, last=True)

            def combine(f):
                with dve.Fori(0, NG) as g:
                    k = g + f * NG
                    step.loop(g, GT)
                    for i in range(GT):
                        dve.wait_ge(residual_in[i], k * 16 + 16)
                        dve.wait_ge(gathered[i], k * 32 + 32)
                        t = g * GT + i
                        for c in range(2):
                            ins = dve.scalar_tensor_tensor(xt[:, i], ga[:, i, c], wgt[:, bass.ds(t, 1), c],
                                                           xt[:, i], ALU.mult, ALU.add)
                            if c == 0:
                                step(ins)
                        ins.then_inc(y_ready[i], 1)
                step.end(NG)

            def retention():
                for n in range(5):
                    dve.wait_ge(aw_hi, n + 1)
                    dve.tensor_tensor(wl[:, n], wst[n % 2], wh[:, n].bitcast(F32), ALU.subtract).then_inc(aw_split, 1)
                dve.wait_ge(small2_in, 16 * 3)
                dve.wait_ge(kz_zeroed, 2)
                with dve.Fori(0, AG) as b:
                    step.loop(b, 6 + KT * 7 + GT)
                    m = b * KT

                    def bank(user, i):
                        return banks[pb[(user, i)] % 2]

                    def query(et):
                        dve.wait_ge(q_full, m + (et + 1))
                        dve.tensor_scalar(qf[:], bank("q", et)[:], cols[:, 0, et:et + 1], float(HD) ** -0.5,
                                          ALU.add, ALU.mult).then_inc(q_evac, 1)
                        dve.wait_ge(q_hi, m + (et + 1))
                        dve.tensor_tensor(ql[:], qf[:], qh[:].bitcast(F32), ALU.subtract).then_inc(q_split, 1)

                    def key_and_gate(et):
                        dve.wait_ge(k_hi, m + (et + 1))
                        for h in range(HPT):
                            r = slice(h * HD, (h + 1) * HD)
                            ins = dve.tensor_tensor(kzl[r, h], kf[r, :], kzh[r, h].bitcast(F32), ALU.subtract)
                        ins.then_inc(k_split, 1)
                        dve.wait_ge(g_exp, m + (et + 1))
                        step(dve.tensor_scalar(tmp[0], egt[:], 1.0, None, ALU.add))
                        dve.tensor_scalar(tmp[1], bank("g", et)[:], cols[:, 2, et:et + 1], None, ALU.add).then_inc(g_evac, 1)
                        step(dve.reciprocal(tmp[0], tmp[0]))
                        step(dve.tensor_tensor(gate[:, et % 2], tmp[1], tmp[0], ALU.mult), wait=False)

                    normalise([(ax_in[i], b * 16 + 16) for i in range(GT)], [axn_ready] * GT, None, b + NG)
                    for i in range(GT):
                        dve.wait_ge(aT_hi, b * GT + (i + 1))
                        dve.tensor_tensor(xTl[:, :, i * P:(i + 1) * P], bank("t", i)[:].rearrange("p (k t) -> p k t", k=KT),
                                          xTh[:, :, i * P:(i + 1) * P].bitcast(F32), ALU.subtract).then_inc(aT_split, 1)
                    for i in range(JT):
                        dve.wait_ge(v_full, b * JT + (i + 1))
                        dve.tensor_tensor(v[:, i], bank("v", i)[:], bvt[:], ALU.add).then_inc(v_ready, 1)
                    query(0)
                    key_and_gate(0)
                    for et in range(KT):
                        dve.wait_ge(d_ready, m + (et + 1))
                        for jt in range(JT):
                            w = S - jt * P
                            dve.wait_ge(pv_done, (m + et) * JT + max(jt - 1, 0))
                            for h in range(HPT):
                                dve.wait_ge(s_full, (m + et) * (JT * HPT) + (jt * HPT + h + 1))
                                dve.tensor_tensor(sc[jt % 2 * HPT + h][:, 0:w], banks[2 + h][:, 0:w], dcy[:, h, 0:w],
                                                  ALU.mult).then_inc(p_ready[h], 1)
                        dve.wait_ge(abs_ready, m + (et + 1))
                        step(dve.tensor_scalar(tmp[0], tmp[0], 1.0, None, ALU.max))
                        step(dve.reciprocal(tmp[0], tmp[0]))
                        dve.tensor_tensor(tmp[1], banks[6][:], tmp[0], ALU.mult).then_inc(a_ready, 1)
                        if et + 1 < KT:
                            query(et + 1)
                        dve.wait_ge(mean_full, m + (et + 1))
                        dve.tensor_tensor(cen[:], tmp[1], bank("mean", et)[:], ALU.subtract).then_inc(centred, 1)
                        if et + 1 < KT:
                            key_and_gate(et + 1)
                        dve.wait_ge(root_ready, m + (et + 1))
                        step(dve.tensor_tensor(tmp[3], cen[:], root, ALU.mult))
                        step(dve.tensor_scalar(tmp[3], tmp[3], cols[:, 3, et:et + 1], cols[:, 4, et:et + 1], ALU.mult, ALU.add))
                        dve.tensor_tensor(tmp[3], tmp[3], gate[:, et % 2], ALU.mult).then_inc(gt_ready, 1)
                        dve.wait_ge(gt_hi, m + (et + 1))
                        dve.tensor_tensor(gtl[:, et], tmp[3], gth[:, et].bitcast(F32), ALU.subtract).then_inc(gt_split, 1)
                    for i in range(GT):
                        dve.wait_ge(o_full, b * GT + (i + 1))
                        step(dve.tensor_tensor(xt[:, i], xt[:, i], bot[:], ALU.add))
                        dve.tensor_tensor(xt[:, i], bank("o", i)[:], xt[:, i], ALU.add).then_inc(x2_ready, 1)
                step.end(AG)

            route(0)
            experts(0)
            combine(0)
            retention()
            route(1)
            experts(1)
            combine(1)

        @block.tensor
        def _(pe):
            pe.wait_ge(const_ready, 6)
            pe.wait_ge(small_in, 16 * 7)
            pe.transpose(out_bank[2][:, 0:P], b1rows, ident[:]).then_inc(biases_turned, 1)
            pe.transpose(out_bank[3][:, 0:5 * KT], colrows, ident[0:5 * KT, 0:5 * KT]).then_inc(biases_turned, 1)

            def turn(dst, src):
                for k in range(KT):
                    ins = pe.transpose(dst[:, k * P:(k + 1) * P], src[:, k * P:(k + 1) * P], ident[:])
                return ins

            def route(f):
                if f:
                    pe.wait_ge(x2_ready, AG * GT)
                with pe.Fori(0, NG) as g:
                    k = g + f * NG

                    def logits(i):
                        pe.wait_ge(xT_copied[i], k + 1)
                        if i == 0:
                            pe.wait_ge(logits_copied, k)
                        for kt in range(KT):
                            ins = pe.matmul(out_bank[0][:, i * NE:(i + 1) * NE], xT[:, i, kt, :], gw[:, kt, :],
                                            start=(kt == 0), stop=(kt == KT - 1))
                        ins.then_inc(logits_full, 1)

                    for i in range(GT):
                        pe.wait_ge(xn_ready[i], k + 1)
                        if i >= 2:
                            pe.wait_ge(xT_copied[i - 2], k + 1)
                        else:
                            pe.wait_ge(xT_copied[i + 2], k)
                        turn(h_bank[i % 2], xn[:, i]).then_inc(xT_full, 1)
                        if i:
                            logits(i - 1)
                    logits(GT - 1)
                    pe.wait_ge(chosen, k + 1)
                    for i in range(GT):
                        pe.matmul(out_bank[1][:, i * NE:(i + 1) * NE], upper[:], ohs[:, i], start=True, stop=(i == 0))
                        for j in range(i):
                            pe.matmul(out_bank[1][:, i * NE:(i + 1) * NE], ones_bf[:], ohs[:, j], start=False, stop=(j == i - 1))
                    for j in range(GT):
                        ins = pe.matmul(out_bank[1][:, GT * NE:(GT + 1) * NE], ones_bf[:], ohs[:, j], start=(j == 0), stop=(j == GT - 1))
                    ins.then_inc(counted, 1)

            def experts(f):
                pe.wait_ge(biases_ready, 2)
                pe.wait_ge(xg_in, f * 16 * (NE + 1) + 16)
                t0 = f * ST * (NE + 1)
                for s in range(ST):
                    if s >= 3:
                        pe.wait_ge(turned_split, t0 + s - 2)
                    turn(h_bank[(s + 2) % 3], xg[:, s]).then_inc(turned, 1)
                with pe.Fori(0, NE) as e:
                    ee = e + f * NE
                    turns = ee * ST + (f * ST + ST)

                    def hidden(n):
                        c, j = n // HPC, n % HPC
                        if j == 0:
                            pe.wait_ge(w1_split[c % RAW], ee * (NC // RAW) + (c // RAW + 1))
                        if n == 0:
                            pe.wait_ge(turned_split, turns)
                        for half in range(2):
                            u = 2 * n + half
                            if u >= 3:
                                pe.wait_ge(h_evac, ee * (2 * HT) + (u - 2))
                            r = slice(half * HALF, (half + 1) * HALF)
                            for kt in range(KT):
                                hi, lo = (w[:, c % SPL, kt, j * P:(j + 1) * P] for w in (w1h, w1l))
                                for i, (w, t) in enumerate(((hi, bTh), (hi, bTl), (lo, bTh))):
                                    ins = pe.matmul(h_bank[u % 3][:, 0:HALF], w, t[:, kt, r],
                                                    start=(kt == 0 and i == 0), stop=(kt == KT - 1 and i == 2))
                            ins.then_inc(h_full, 1)
                            last = ins
                        return last

                    def output(n):
                        c, j = n // HPC, n % HPC
                        pe.wait_ge(h_split, ee * HT + (n + 1))
                        if j == 0:
                            pe.wait_ge(w2_split[c % RAW], ee * (NC // RAW) + (c // RAW + 1))
                        if n == 0:
                            pe.wait_ge(o_ready, ee * ST)
                        for s in range(ST):
                            hi, lo = (t[:, n % 4, s * P:(s + 1) * P] for t in (hh, hl))
                            for i, (t, w) in enumerate(((hi, w2h), (hi, w2l), (lo, w2h))):
                                ins = pe.matmul(out_bank[s][:], t, w[:, c % SPL, j, :],
                                                start=(n == 0 and i == 0), stop=(n == HT - 1 and i == 2))
                        ins.then_inc(b_done, 1)

                    def turn_next(s):
                        if s == 0:
                            pe.wait_ge(xg_in, ee * 16 + (f * 16 + 32))
                        if s < 3:
                            pe.wait_ge(h_evac, ee * (2 * HT) + (2 * HT - 2 + s))
                        else:
                            pe.wait_ge(turned_split, turns + (s - 2))
                        turn(h_bank[(s + 2) % 3], xg[:, s]).then_inc(turned, 1)

                    for n in range(HT):
                        hidden(n)
                        if n >= 2:
                            output(n - 2)
                    for s in range(3):
                        turn_next(s)
                    output(HT - 2)
                    for s in range(3, ST):
                        turn_next(s)
                    output(HT - 1)

            def retention():
                pe.wait_ge(aw_split, 5)
                with pe.Fori(0, AG) as b:
                    m = b * KT
                    freed = {}
                    for i in range(GT):
                        freed["t", i], freed["v", i] = (aT_split, GT, i + 1), (v_ready, JT, i + 1)
                        freed["o", i] = (x2_ready, GT, i + 1)
                    for et in range(KT):
                        freed["q", et], freed["k", et], freed["g", et] = (q_evac, KT, et + 1), (k_evac, KT, et + 1), (g_evac, KT, et + 1)
                        freed["mean", et], freed["var", et] = (centred, KT, et + 1), (var_read, KT, et + 1)

                    def bank(user, i):
                        n = pb[(user, i)]
                        if n >= 2:
                            s, per, c = freed[order[n - 2]]
                            pe.wait_ge(s, b * per + c)
                        else:
                            pe.wait_ge(x2_ready, b * GT)
                        return banks[n % 2]

                    def three(dst, pairs):
                        for n, ((sh, sl), (mh, ml)) in enumerate(pairs):
                            first, final = n == 0, n == len(pairs) - 1
                            pe.matmul(dst, sh, mh, start=first, stop=False)
                            pe.matmul(dst, sh, ml, start=False, stop=False)
                            ins = pe.matmul(dst, sl, mh, start=False, stop=final)
                        return ins

                    def project(user, w, et, done):
                        cs = slice(et * P, (et + 1) * P)
                        three(bank(user, et)[:], [((wh[:, w, kt, cs], wl[:, w, kt, cs]), (xTh[:, kt], xTl[:, kt]))
                                                  for kt in range(KT)]).then_inc(done, 1)

                    for i in range(GT):
                        pe.wait_ge(axn_ready, b * GT + (i + 1))
                        turn(bank("t", i), xn[:, i]).then_inc(aT_full, 1)
                    for i in range(JT):
                        pe.wait_ge(aT_split, b * GT + (i + 1))
                        ts = slice(i * P, (i + 1) * P)
                        three(bank("v", i)[:], [((xTh[:, kt, ts], xTl[:, kt, ts]), (wh[:, 2, kt], wl[:, 2, kt]))
                                                for kt in range(KT)]).then_inc(v_full, 1)
                    project("q", 0, 0, q_full)
                    project("k", 1, 0, k_full)
                    project("g", 3, 0, g_full)
                    for et in range(KT):
                        pe.wait_ge(q_split, m + (et + 1))
                        pe.wait_ge(k_split, m + (et + 1))
                        if et == 0:
                            pe.wait_ge(v_ready, b * JT + JT)

                        def scores(jt):
                            for h in range(HPT):
                                pe.wait_ge(p_ready[h], (m + et) * JT + jt)
                                ks = slice(jt * P, (jt + 1) * P)
                                three(banks[2 + h][:, 0:S - jt * P], [((kzh[:, h, ks], kzl[:, h, ks]), (qh[:, jt * P:S], ql[:, jt * P:S]))]
                                      ).then_inc(s_full, 1)

                        def values(jt):
                            if jt == 0:
                                pe.wait_ge(a_ready, m + et)
                            for h in range(HPT):
                                pe.wait_ge(p_ready[h], (m + et) * JT + (jt + 1))
                            for dst, ones in ((banks[6], False), (banks[7], True)):
                                for h in range(HPT):
                                    hd = et * HPT + h
                                    lhsT = ones32[:] if ones else v[:, jt, hd * HD:(hd + 1) * HD]
                                    ins = pe.matmul(dst[h * HD:(h + 1) * HD, jt * P:S], lhsT, sc[jt % 2 * HPT + h][:, 0:S - jt * P],
                                                    start=(jt == 0), stop=(jt == JT - 1))
                            ins.then_inc(pv_done, 1)

                        scores(0)
                        for jt in range(1, JT):
                            scores(jt)
                            values(jt - 1)
                        values(JT - 1)
                        if et + 1 < KT:
                            project("q", 0, et + 1, q_full)
                        mean = bank("mean", et)
                        pe.wait_ge(a_ready, m + (et + 1))
                        pe.matmul(mean[:], headmean[:], tmp[1], start=True, stop=True).then_inc(mean_full, 1)
                        if et + 1 < KT:
                            project("k", 1, et + 1, k_full)
                            project("g", 3, et + 1, g_full)
                        spread = bank("var", et)
                        pe.wait_ge(squared, m + (et + 1))
                        pe.matmul(spread[:], headmean[:], tmp[2], start=True, stop=True).then_inc(var_full, 1)
                    pe.wait_ge(gt_split, m + KT)
                    for i in range(GT):
                        ts = slice(i * P, (i + 1) * P)
                        three(bank("o", i)[:], [((gth[:, kt, ts], gtl[:, kt, ts]), (wh[:, 4, kt], wl[:, 4, kt]))
                                                for kt in range(KT)]).then_inc(o_full, 1)

            route(0)
            experts(0)
            retention()
            route(1)
            experts(1)


_INS = ['L0_attn_x', 'L0_attn_Wq', 'L0_attn_bq', 'L0_attn_Wk', 'L0_attn_bk', 'L0_attn_Wv', 'L0_attn_bv', 'L0_attn_Wg',
        'L0_attn_bg', 'L0_attn_Wo', 'L0_attn_bo', 'L0_attn_gn_w', 'L0_attn_gn_b', 'L0_attn_decay', 'L0_ffn_gating_w',
        'L0_ffn_w1', 'L0_ffn_b1', 'L0_ffn_w2', 'L0_ffn_b2']
_OUTS = [((4, 512, 512), 'float32')]


def kernel(**inputs):
    import numpy as _np
    import concourse.bacc as _bacc
    from concourse import mybir as _mybir
    from concourse.bass_utils import run_bass_kernel_spmd as _run

    nc = _bacc.Bacc("TRN2", target_bir_lowering=False, num_devices=1)
    arrays, args = {}, []
    for name in _INS:
        a = _np.ascontiguousarray(inputs[name])
        arrays[f"in_{name}_dram"] = a
        args.append(nc.dram_tensor(f"in_{name}_dram", a.shape, _mybir.dt.from_np(a.dtype), kind="ExternalInput").ap())
    for i, (shape, dtype) in enumerate(_OUTS):
        dt = _mybir.dt.from_np(_np.dtype(dtype))
        args.append(nc.dram_tensor(f"out_{i}_dram", shape, dt, kind="ExternalOutput").ap())
    macaron_program(nc, *args)
    r = _run(nc, [arrays], core_ids=[0])
    got = tuple(r.results[0][f"out_{i}_dram"] for i in range(len(_OUTS)))
    return got[0]
```

```python
from contextlib import ExitStack

import concourse.bass as bass
from concourse import mybir

ALU = mybir.AluOpType
ACT = mybir.ActivationFunctionType
AX_X = mybir.AxisListType.X
F32 = mybir.dt.float32
F32R = mybir.dt.float32r
BF16 = mybir.dt.bfloat16
U32 = mybir.dt.uint32

P = 128


class Steps:

    def __init__(self, eng, sem):
        self.eng, self.sem, self.base, self.n = eng, sem, 0, 0

    def loop(self, i, per):
        self.start, self.per, self.n = self.base + self.n, per, 0
        self.base = self.start + i * per

    def end(self, trips):
        assert self.n == self.per, (self.n, self.per)
        self.base, self.n = self.start + trips * self.per, 0

    def __call__(self, ins, wait=True):
        ins.then_inc(self.sem, 1)
        self.n += 1
        if wait:
            self.eng.wait_ge(self.sem, self.base + self.n)


def macaron_program(nc, x, Wq, bq, Wk, bk, Wv, bv, Wg, bg, Wo, bo, gn_w, gn_b, decay, gating_w, w1, b1, w2, b2, out):
    B, S, E = x.shape
    T = B * S
    NT = T // P
    KT = E // P
    NE, _, HID = w1.shape
    NG, GT = NT // 4, 4
    CAP = -(-(T * 2) * 5 // (NE * 4))
    ST = CAP // P
    HALF = CAP // 2
    HT = HID // P
    HPC = 2
    NC = HT // HPC
    CW = HPC * P
    RAW, SPL = 4, 2
    H = decay.shape[0]
    HD = E // H
    HPT = P // HD
    JT = S // P
    EPS = 1e-5
    FAR = 65536.0
    assert (NT, KT, ST, HALF, NE, HPT, JT, GT) == (16, 4, 5, 320, 8, 4, 4, 4)

    x_rows = x.rearrange("b s e -> (b s) e")
    out_rows = out.rearrange("b s e -> (b s) e")
    xbuf = nc.dram_tensor("xbuf", [(NE + 1) * CAP, E], F32).ap()
    obuf = nc.dram_tensor("obuf", [NE * CAP, E], F32).ap()
    x1_rows = nc.dram_tensor("x1", [T, E], F32).ap()
    x2_rows = nc.dram_tensor("x2", [T, E], F32).ap()

    with ExitStack() as ctx:
        def sb(name, shape, dt=F32, stack=ctx):
            return stack.enter_context(nc.sbuf_tensor(name, shape, dt))

        def sem(name):
            return ctx.enter_context(nc.semaphore(name))

        def sems(name, n):
            return [sem(f"{name}{i}") for i in range(n)]

        banks = [ctx.enter_context(nc.psum_tensor(f"bank{i}", [P, 512], F32)) for i in range(8)]
        out_bank, h_bank = banks[0:5], banks[5:8]

        ident = sb("ident", [P, P])
        upper = sb("upper", [P, P], BF16)
        ones_bf = sb("ones_bf", [P, P], BF16)
        ones32 = sb("ones32", [P, HD])
        headmean = sb("headmean", [P, P])
        iota8 = sb("iota8", [P, NE])
        slot0 = sb("slot0", [P, GT, NE])
        b1T = sb("b1T", [P, NE * HT])
        gw = sb("gw", [P, KT, NE])
        b1e = sb("b1e", [P, HT])
        cols = sb("cols", [P, 6, KT])
        centre = sb("centre", [P, P])
        mv = sb("mv", [P, GT, 2])
        st6 = sb("st6", [P, GT, 6])
        var = sb("var", [P, GT])
        rstd = sb("rstd", [P, GT])
        newton = sb("newton", [P, GT])
        lg = sb("lg", [P, GT, NE])
        mx = sb("mx", [P, GT])
        ex = sb("ex", [P, GT, NE])
        sm = sb("sm", [P, GT])
        gates = sb("gates", [P, GT, NE])
        top = sb("top", [P, GT, 8])
        topi = sb("topi", [P, GT, 8], U32)
        topf = sb("topf", [P, GT, 2])
        oh = sb("oh", [P, GT, 2, NE])
        ohs = sb("ohs", [P, GT, NE], BF16)
        carry = sb("carry", [P, NE])
        count = sb("count", [P, GT, NE])
        gslot = sb("gslot", [P, GT, NE])
        sslot = sb("sslot", [P, GT, NE])
        pick = sb("pick", [P, GT, 2, NE])
        scf = sb("scf", [P, GT, 2])
        gaf = sb("gaf", [P, GT, 2])
        sci = sb("sci", [P, GT, 2], U32)
        tsum = sb("tsum", [P, GT])
        wk2 = sb("wk2", [P, GT, 2])
        vld = sb("vld", [P, GT, 2])
        gidx = sb("gidx", [P, NT, 2], U32)
        wgt = sb("wgt", [P, NT, 2])
        cidx = sb("cidx", [P, GT, 2], U32)
        xt = sb("xt", [P, GT, E])
        xn = sb("xn", [P, GT, E])
        xT = sb("xT", [P, GT, KT, P])
        ga = sb("ga", [P, GT, 2, E])
        b1rows, colrows = xT[:, 0, 0, :], xT[0:5 * KT, 1, 0, :]

        with ExitStack() as ffn:
            w1raw = sb("w1raw", [P, RAW, KT, CW], F32, ffn)
            w2raw = sb("w2raw", [P, RAW, HPC, E], F32, ffn)
            w1h = sb("w1h", [P, SPL, KT, CW], F32R, ffn)
            w1l = sb("w1l", [P, SPL, KT, CW], F32R, ffn)
            w2h = sb("w2h", [P, SPL, HPC, E], F32R, ffn)
            w2l = sb("w2l", [P, SPL, HPC, E], F32R, ffn)
            bTh = sb("bTh", [P, KT, CAP], F32R, ffn)
            bTl = sb("bTl", [P, KT, CAP], F32R, ffn)
            xg = sb("xg", [P, ST, E], F32, ffn)
            hf = sb("hf", [P, 2, CAP], F32, ffn)
            hh = sb("hh", [P, 4, CAP], F32R, ffn)
            hl = sb("hl", [P, 4, CAP], F32R, ffn)
            o = sb("o", [P, ST, E], F32, ffn)
            b2t = sb("b2t", [P, E], F32, ffn)
        with ExitStack() as att:
            wh = sb("wh", [P, 5, KT, E], F32R, att)
            wl = sb("wl", [P, 5, KT, E], F32R, att)
            xTh = sb("xTh", [P, KT, S], F32R, att)
            xTl = sb("xTl", [P, KT, S], F32R, att)
            pf = sb("pf", [P, S], F32, att)
            qh = sb("qh", [P, S], F32R, att)
            ql = sb("ql", [P, S], F32R, att)
            kzh = sb("kzh", [P, HPT, S], F32R, att)
            kzl = sb("kzl", [P, HPT, S], F32R, att)
            v = sb("v", [P, JT, E], F32, att)
            dcy = sb("dcy", [P, HPT, S], F32, att)
            dif = sb("dif", [P, S], F32, att)
            gate = sb("gate", [P, 2, S], F32, att)
            gth = sb("gth", [P, KT, S], F32R, att)
            gtl = sb("gtl", [P, KT, S], F32R, att)
            bvt = sb("bvt", [P, E], F32, att)
            bot = sb("bot", [P, E], F32, att)
            dect = sb("dect", [P, H], F32, att)
        with ExitStack() as raw:
            sb("beside_wh", [P, 5, KT, E], F32, raw)
            wraw = sb("wraw", [P, 5, KT, E], F32, raw)
        tmp = [xT[:, i, :, :].rearrange("p k t -> p (k t)") for i in range(GT)]
        spread, norm, denom, sig = tmp
        sc = [ga[:, i // 2, i % 2, :] for i in range(2 * GT)]

        const_ready = sem("const_ready")
        pool_step = sem("pool_step")
        dve_step = sem("dve_step")
        zero_ready = sem("zero_ready")
        zero_filled = sem("zero_filled")
        small_in = sem("small_in")
        biases_turned, biases_ready, b1e_ready = sem("biases_turned"), sem("biases_ready"), sem("b1e_ready")
        x_in = sems("x_in", GT)
        var_ready, ln_ready, rstd_ready = sem("var_ready"), sem("ln_ready"), sem("rstd_ready")
        xn_ready = sem("xn_ready")
        xT_full = sem("xT_full")
        xT_copied = sem("xT_copied")
        logits_full = sem("logits_full")
        logits_copied = sem("logits_copied")
        shifted = sem("shifted")
        exp_ready = sem("exp_ready")
        chosen = sem("chosen")
        counted = sem("counted")
        slots_ready = sem("slots_ready")
        scattered = sems("scattered", GT)
        w1_in, w2_in = sems("w1_in", RAW), sems("w2_in", RAW)
        w1_hi, w2_hi = sem("w1_hi"), sem("w2_hi")
        w1_split, w2_split = sems("w1_split", RAW), sems("w2_split", RAW)
        xg_in, b2_in = sem("xg_in"), sem("b2_in")
        turned, turned_hi, turned_split = sem("turned"), sem("turned_hi"), sem("turned_split")
        h_full, h_evac, h_hi, h_split = sem("h_full"), sem("h_evac"), sem("h_hi"), sem("h_split")
        b_done, o_ready = sem("b_done"), sem("o_ready")
        o_stored = sems("o_stored", ST)
        cidx_ready = sem("cidx_ready")
        gathered = [sems(f"choice{c}_gathered", GT) for c in range(2)]
        residual_in = sems("residual_in", GT)
        y_ready = sems("y_ready", GT)
        y_stored = sems("y_stored", GT)
        aw_in = sems("aw_in", 5)
        aw_hi, aw_split = sem("aw_hi"), sem("aw_split")
        small2_in = sem("small2_in")
        cols_ready, kz_zeroed, dif_ready = sem("cols_ready"), sem("kz_zeroed"), sem("dif_ready")
        folded = sem("folded")
        axn_ready = sem("axn_ready")
        aT_full, aT_hi, aT_split = sem("aT_full"), sem("aT_hi"), sem("aT_split")
        v_full, v_ready = sem("v_full"), sem("v_ready")
        q_full, q_evac, q_hi, q_split = sem("q_full"), sem("q_evac"), sem("q_hi"), sem("q_split")
        k_full, k_evac, k_hi, k_split = sem("k_full"), sem("k_evac"), sem("k_hi"), sem("k_split")
        g_full, g_exp, g_evac = sem("g_full"), sem("g_exp"), sem("g_evac")
        denom_ready, sig_ln, sig_ready, gated = sem("denom_ready"), sem("sig_ln"), sem("sig_ready"), sem("gated")
        d_exp, d_ready = sem("d_exp"), sem("d_ready")
        s_full = sem("s_full")
        p_ready = sem("p_ready")
        pv_done = sem("pv_done")
        a_copied, sum_squared, centred, squared = sem("a_copied"), sem("sum_squared"), sem("centred"), sem("squared")
        var_full, var_summed, root_ln, root_ready = sem("var_full"), sem("var_summed"), sem("root_ln"), sem("root_ready")
        scaled, gt_ready, gt_hi, gt_split = sem("scaled"), sem("gt_ready"), sem("gt_hi"), sem("gt_split")
        o_full, x2_ready = sem("o_full"), sem("x2_ready")
        ax_in, res_ready = sems("ax_in", GT), sem("res_ready")
        x2_stored = sems("x2_stored", GT)
        waits_carried = sem("waits_carried")

        def carry_wait(eng):
            eng.sem_inc(waits_carried, 1)

        block = ctx.enter_context(nc.Block())
        AG = NG

        heads_bank, sums_bank = banks[6], banks[7]
        WQ, WK, WV, WG, WO = range(5)
        weight_order = (WV, WQ, WK, WG, WO)

        def turn_bank(user, i):
            first = {"t": 0, "v": 0, "o": 1, "q": 0, "k": 1, "g": 0}[user]
            return (first + (i if user in "tvo" else 3 * i)) % 2

        @block.sync
        def _(sp):
            sp.dma_start(gw[:], gating_w.rearrange("(k p) e -> p k e", p=P)).then_inc(small_in, 16)
            sp.dma_start(b1rows, b1.rearrange("e (t p) -> (e t) p", p=P)).then_inc(small_in, 16)
            for n, src in enumerate((bq, bk, bg, gn_w, gn_b)):
                sp.dma_start(colrows[n * KT:(n + 1) * KT, :], src.rearrange("(k p) -> k p", p=P)).then_inc(small_in, 16)

            def route_loads(f, src):
                if f:
                    for i in range(GT):
                        sp.wait_ge(x2_stored[i], 16 * AG)
                with sp.Fori(0, NG) as g:
                    for i in range(GT):
                        if i == 0:
                            sp.wait_ge(xn_ready, g * GT + f * NG * GT)
                        sp.dma_start(xt[:, i, :], src[bass.ds((g * GT + i) * P, P), :]).then_inc(x_in[i], 16)

            def expert_loads(f):
                with sp.Fori(0, NE) as e:
                    ee = e + f * NE
                    for c in range(NC):
                        r, uses = c % RAW, ee * (NC // RAW) + c // RAW
                        sp.wait_ge(w1_split[r], uses)
                        sp.dma_start(w1raw[:, r], w1[bass.ds(e, 1), :, c * CW:(c + 1) * CW].rearrange(
                            "o (k p) n -> p (o k) n", p=P)).then_inc(w1_in[r], 16)
                        sp.wait_ge(w2_split[r], uses)
                        sp.dma_start(w2raw[:, r], w2[bass.ds(e, 1), c * CW:(c + 1) * CW, :].rearrange(
                            "o (t p) n -> p (o t) n", p=P)).then_inc(w2_in[r], 16)

            def combine_moves(f, src, dst):
                with sp.Fori(0, NG) as g:
                    k = g + f * NG
                    for i in range(GT):
                        sp.wait_ge(y_stored[i], 16 * k)
                        sp.dma_start(xt[:, i, :], src[bass.ds((g * GT + i) * P, P), :]).then_inc(residual_in[i], 16)
                    for i in range(GT):
                        sp.wait_ge(y_ready[i], k + 1)
                        sp.dma_start(dst[bass.ds((g * GT + i) * P, P), :], xt[:, i, :]).then_inc(y_stored[i], 16)

            def retention_moves():
                def residual(b, done):
                    sp.wait_ge(axn_ready, b * GT)
                    carry_wait(sp)
                    for i in range(GT):
                        sp.wait_ge(y_stored[i], 16 * b)
                        carry_wait(sp)
                        sp.wait_ge(x2_stored[i], 16 * done)
                        carry_wait(sp)
                        sp.dma_start(xt[:, i, :], x_rows[bass.ds((b * GT + i) * P, P), :]).then_inc(residual_in[i], 16)

                def store_sum(b):
                    for i in range(GT):
                        sp.wait_ge(y_ready[i], b + 1)
                        carry_wait(sp)
                        sp.dma_start(x1_rows[bass.ds((b * GT + i) * P, P), :], xt[:, i, :]).then_inc(y_stored[i], 16)

                def body(b, last=False):
                    if not last:
                        residual(b + 1, b)
                        store_sum(b + 1)
                        sp.wait_ge(axn_ready, (b + 2) * GT)
                        carry_wait(sp)
                    for i in range(GT):
                        if last:
                            sp.wait_ge(x2_stored[i], 16 * b)
                        else:
                            sp.wait_ge(y_stored[i], 16 * (b + 2))
                        carry_wait(sp)
                        sp.dma_start(xt[:, i, :], x1_rows[bass.ds((b * GT + i) * P, P), :]).then_inc(ax_in[i], 16)
                    for i in range(GT):
                        sp.wait_ge(x2_ready, b * GT + i + 1)
                        carry_wait(sp)
                        sp.dma_start(x2_rows[bass.ds((b * GT + i) * P, P), :], xt[:, i, :]).then_inc(x2_stored[i], 16)

                for t, src in ((bvt, bv), (bot, bo), (dect, decay)):
                    sp.dma_start(t[:], src.rearrange("(a n) -> a n", a=1).broadcast_to(t.shape)).then_inc(small2_in, 16)
                residual(0, 0)
                sp.wait_ge(b_done, HT * NE)
                sp.wait_ge(turned_split, ST * (NE + 1))
                for j, n in enumerate(weight_order):
                    sp.dma_start(wraw[:, n], (Wq, Wk, Wv, Wg, Wo)[n].rearrange("(k p) n -> p k n", p=P)).then_inc(aw_in[j], 16)
                store_sum(0)
                with sp.Fori(0, AG - 1) as b:
                    body(b)
                body(AG - 1, last=True)

            route_loads(0, x_rows)
            expert_loads(0)
            retention_moves()
            route_loads(1, x2_rows)
            expert_loads(1)
            combine_moves(1, x2_rows, out_rows)
            for i in range(GT):
                sp.wait_ge(y_stored[i], 16 * 2 * NG)

        @block.gpsimd
        def _(pool):
            step = Steps(pool, pool_step)
            pool.memset(ga[:, 0, 0, :], 0.0).then_inc(zero_ready, 1)
            step(pool.memset(ident[:], 0.0), wait=False)
            step(pool.memset(upper[:], 1.0), wait=False)
            step(pool.memset(headmean[:], 1.0 / HD), wait=False)
            step(pool.iota(iota8[:], [[1, NE]], base=0, channel_multiplier=0,
                           allow_small_or_imprecise_dtypes=True), wait=False)
            step(pool.iota(slot0[:], [[0, GT], [CAP, NE]], base=0, channel_multiplier=0,
                           allow_small_or_imprecise_dtypes=True))
            pool.affine_select(out=ident[:], in_=ident[:], compare_op=ALU.not_equal, fill=1.0,
                               base=0, pattern=[[-1, P]], channel_multiplier=1).then_inc(const_ready, 1)
            pool.affine_select(out=upper[:], in_=upper[:], compare_op=ALU.is_gt, fill=0.0,
                               base=0, pattern=[[1, P]], channel_multiplier=-1).then_inc(const_ready, 1)
            hm = headmean[:].rearrange("p (h d) -> p h d", d=HD)
            step(pool.affine_select(out=hm, in_=hm, compare_op=ALU.is_ge, fill=0.0,
                                    base=0, pattern=[[-HD, HPT], [0, HD]], channel_multiplier=1))
            pool.affine_select(out=hm, in_=hm, compare_op=ALU.is_ge, fill=0.0,
                               base=HD - 1, pattern=[[HD, HPT], [0, HD]], channel_multiplier=-1).then_inc(const_ready, 1)
            pool.wait_ge(const_ready, 3)
            pool.tensor_tensor(centre[:], ident[:], headmean[:], ALU.subtract).then_inc(const_ready, 1)
            pool.memset(ones_bf[:], 1.0).then_inc(const_ready, 1)
            pool.memset(ones32[:], 1.0).then_inc(const_ready, 1)
            pool.memset(carry[:], 0.0).then_inc(const_ready, 1)

            bound = pool.to_reg(NE * CAP - 1)
            zero = pool.to_reg(0.0)

            def scatter(f):
                if f == 0:
                    pool.wait_ge(zero_filled, 16 * 3)
                with pool.Fori(0, NG) as g:
                    pool.wait_ge(slots_ready, f * NG + g + 1)
                    carry_wait(pool)
                    for i in range(GT):
                        for c in range(2):
                            pool.indirect_dma_start(
                                out=xbuf, out_offset=bass.IndirectOffsetOnAxis(ap=sci[:, i, c:c + 1], axis=0),
                                in_=xn[:, i, :], in_offset=None, bounds_check=bound,
                                oob_is_err=False).then_inc(scattered[i], 16)

            def load_expert_rows(e, used):
                pool.wait_ge(turned, used)
                pool.dma_start(xg[:], xbuf[bass.ds(e * CAP, CAP), :].rearrange(
                    "(s p) d -> p s d", p=P)).then_inc(xg_in, 16)

            def expert_moves(f):
                for i in range(GT):
                    pool.wait_ge(scattered[i], 32 * NG * (f + 1))
                load_expert_rows(0, f * ST * (NE + 1))
                with pool.Fori(0, NE) as e:
                    ee = e + f * NE
                    pool.wait_ge(o_ready, ee * ST)
                    pool.dma_start(b2t[:], b2[bass.ds(e, 1), :].broadcast_to([P, E])).then_inc(b2_in, 16)
                    load_expert_rows(e + 1, e * ST + (f * ST * (NE + 1) + ST))
                    for s in range(ST):
                        pool.wait_ge(o_ready, ee * ST + s + 1)
                        pool.dma_start(obuf[bass.ds(e * CAP + s * P, P), :], o[:, s, :]).then_inc(o_stored[s], 16)

            def gather(f):
                for s in range(ST):
                    pool.wait_ge(o_stored[s], 16 * NE * (f + 1))
                with pool.Fori(0, NG) as g:
                    k = g + f * NG
                    for i in range(GT):
                        pool.wait_ge(y_ready[i], k)
                    pool.tensor_copy(cidx[:], gidx[:, bass.ds(g * GT, GT), :]).then_inc(cidx_ready, 1)
                    pool.wait_ge(cidx_ready, k + 1)
                    carry_wait(pool)
                    for i in range(GT):
                        for c in range(2):
                            pool.indirect_dma_start(
                                out=ga[:, i, c, :], out_offset=None, in_=obuf,
                                in_offset=bass.IndirectOffsetOnAxis(ap=cidx[:, i, c:c + 1], axis=0),
                                bounds_check=bound, oob_is_err=False).then_inc(gathered[c][i], 16)

            def retention():
                def gather_half(b, c, dst):
                    if c == 0:
                        pool.tensor_copy(cidx[:], gidx[:, bass.ds(b * GT, GT), :]).then_inc(cidx_ready, 1)
                        pool.wait_ge(cidx_ready, b + 1)
                        carry_wait(pool)
                    for i in range(GT):
                        pool.indirect_dma_start(
                            out=dst[i], out_offset=None, in_=obuf,
                            in_offset=bass.IndirectOffsetOnAxis(ap=cidx[:, i, c:c + 1], axis=0),
                            bounds_check=bound, oob_is_err=False).then_inc(gathered[c][i], 16)

                def mask(f):
                    pool.wait_ge(d_exp, f + 1)
                    carry_wait(pool)
                    for h in range(HPT):
                        m = pool.affine_select(out=dcy[:, h, 0:P], in_=dcy[:, h, 0:P], compare_op=ALU.is_ge,
                                               fill=zero, base=0, pattern=[[1, P]], channel_multiplier=-1)
                    m.then_inc(d_ready, 1)

                rows = [xn[:, i] for i in range(GT)]

                def body(b, last=False):
                    m = b * KT
                    for et in range(KT):
                        if et == 0 and not last:
                            pool.wait_ge(aT_full, (b + 1) * GT)
                            gather_half(b + 1, 0, rows)
                        if et == 1 and not last:
                            pool.wait_ge(folded, (b + 2) * GT)
                            carry_wait(pool)
                            gather_half(b + 1, 1, rows)
                        if et == KT - 1:
                            for i in range(GT):
                                pool.wait_ge(ax_in[i], 16 * (b + 1))
                                pool.tensor_tensor(xt[:, i], xt[:, i], bot[:], ALU.add).then_inc(res_ready, 1)
                        if et < KT - 1 or not last:
                            mask(m + (et + 1))

                for s in range(ST):
                    pool.wait_ge(o_stored[s], 16 * NE)
                gather_half(0, 0, rows)
                gather_half(0, 1, sc)
                pool.memset(kzh[:].bitcast(U32), 0).then_inc(kz_zeroed, 1)
                pool.memset(kzl[:].bitcast(U32), 0).then_inc(kz_zeroed, 1)
                step(pool.iota(dif[:], [[1, S]], base=0, channel_multiplier=-1,
                               allow_small_or_imprecise_dtypes=True))
                pool.tensor_scalar(dif[:], dif[:], 0.0, None, ALU.max).then_inc(dif_ready, 1)
                pool.wait_ge(small2_in, 16 * 3)
                mask(0)
                with pool.Fori(0, AG - 1) as b:
                    body(b)
                body(AG - 1, last=True)

            scatter(0)
            expert_moves(0)
            retention()
            scatter(1)
            expert_moves(1)
            gather(1)

        @block.scalar
        def _(act):
            act.preload_act_table_set("natural_log_exp_and_others")
            act.wait_ge(zero_ready, 1)
            rows = (NE + 1) * CAP // 3
            for n in range(3):
                act.dma_start(xbuf[n * rows:(n + 1) * rows, :].rearrange("(t p) d -> p t d", p=P),
                              ga[:, 0, 0:1, :].broadcast_to([P, rows // P, E])).then_inc(zero_filled, 16)

            def inverse_root(groups):
                act.wait_ge(var_ready, groups + 1)
                act.activation(rstd[:], var[:], ACT.Ln).then_inc(ln_ready, 1)
                act.wait_ge(ln_ready, groups + 1)
                act.activation(rstd[:], rstd[:], ACT.Exp, scale=-0.5).then_inc(rstd_ready, 1)

            def route(f):
                with act.Fori(0, NG) as g:
                    k = g + f * NG
                    inverse_root(k + f * AG)
                    act.wait_ge(logits_full, k * GT)
                    for i in range(GT):
                        act.wait_ge(xT_full, k * GT + (i + 1))
                        act.activation(xT[:, i].rearrange("p k t -> p (k t)"), h_bank[i % 2][:], ACT.Copy).then_inc(xT_copied, 1)
                    act.wait_ge(shifted, k + 1)
                    act.activation(ex[:], lg[:], ACT.Exp).then_inc(exp_ready, 1)

            def turn_evac(base):
                for s in range(ST):
                    act.wait_ge(turned, base + (s + 1))
                    act.activation(bTh[:, :, s * P:(s + 1) * P], h_bank[(s + 2) % 3][:].rearrange("p (k t) -> p k t", k=KT),
                                   ACT.Copy).then_inc(turned_hi, 1)

            def experts(f):
                def body(e, first_weights=False, last=False):
                    ee = e + f * NE

                    def split_w1(c):
                        act.wait_ge(w1_in[c % RAW], 16 * (c // RAW + 1) + ee * (16 * NC // RAW))
                        act.wait_ge(h_full, ee * (2 * HT) + max((c - SPL + 1) * 2 * HPC, 0))
                        act.activation(w1h[:, c % SPL], w1raw[:, c % RAW], ACT.Copy).then_inc(w1_hi, 1)

                    def split_w2(c):
                        act.wait_ge(w2_in[c % RAW], 16 * (c // RAW + 1) + ee * (16 * NC // RAW))
                        act.wait_ge(b_done, ee * HT + max((c - SPL + 1) * HPC, 0))
                        act.activation(w2h[:, c % SPL], w2raw[:, c % RAW], ACT.Copy).then_inc(w2_hi, 1)

                    if first_weights:
                        split_w1(0)
                        split_w1(1)
                        split_w2(0)
                        return
                    act.activation(b1e[:], b1T[:, bass.ds(e * HT, HT)], ACT.Copy).then_inc(b1e_ready, 1)
                    act.wait_ge(b1e_ready, ee + 1)
                    for n in range(HT):
                        if n in (0, 1):
                            act.wait_ge(h_split, ee * HT)
                        else:
                            act.wait_ge(h_split, ee * HT + (n - 1))
                        for half in range(2):
                            act.wait_ge(h_full, ee * (2 * HT) + (2 * n + half + 1))
                            act.activation(hf[:, n % 2, half * HALF:(half + 1) * HALF], h_bank[(2 * n + half) % 3][:, 0:HALF],
                                           ACT.Relu, bias=b1e[:, n:n + 1]).then_inc(h_evac, 1)
                        act.wait_ge(h_evac, ee * (2 * HT) + (2 * n + 2))
                        act.wait_ge(b_done, ee * HT + max(n - 3, 0))
                        act.activation(hh[:, n % 4], hf[:, n % 2], ACT.Copy).then_inc(h_hi, 1)
                        if n % 2 == 1:
                            c = n // 2
                            if c + 2 < NC or not last:
                                split_w1(c + 2)
                            if c + 1 < NC or not last:
                                split_w2(c + 1)
                    turn_evac(ee * ST + (f * ST + ST))

                body(0, first_weights=True)
                turn_evac(f * ST * (NE + 1))
                with act.Fori(0, NE - 1) as e:
                    body(e)
                body(NE - 1, last=True)

            def retention():
                def weight_hi(j):
                    act.wait_ge(aw_in[j], 16)
                    n = weight_order[j]
                    act.activation(wh[:, n], wraw[:, n], ACT.Copy).then_inc(aw_hi, 1)

                def turned_hi_part(b, i):
                    act.wait_ge(aT_full, b * GT + (i + 1))
                    act.activation(xTh[:, :, i * P:(i + 1) * P], banks[turn_bank("t", i)][:].rearrange("p (k t) -> p k t", k=KT),
                                   ACT.Copy).then_inc(aT_hi, 1)

                def query(m):
                    act.wait_ge(q_evac, m + 1)
                    act.activation(qh[:], pf[:], ACT.Copy).then_inc(q_hi, 1)

                def decays(m, et):
                    act.wait_ge(p_ready, m * (JT * HPT))
                    for h in range(HPT):
                        hd = et * HPT + h
                        ins = act.activation(dcy[:, h], dif[:], ACT.Exp, scale=dect[:, hd:hd + 1])
                    ins.then_inc(d_exp, 1)

                def key(m):
                    act.wait_ge(k_evac, m + 1)
                    for h in range(HPT):
                        r = slice(h * HD, (h + 1) * HD)
                        act.activation(kzh[r, h], pf[r, :], ACT.Copy).then_inc(k_hi, 1)

                def gate_exp(m, et):
                    act.wait_ge(g_full, m + 1)
                    act.wait_ge(gated, m)
                    act.activation(denom, banks[turn_bank("g", et)][:], ACT.Exp, scale=-1.0,
                                   bias=cols[:, 5, et:et + 1]).then_inc(g_exp, 1)

                def gate_inverse(m):
                    act.wait_ge(denom_ready, m + 1)
                    act.activation(sig, denom, ACT.Ln).then_inc(sig_ln, 1)
                    act.wait_ge(sig_ln, m + 1)
                    act.activation(sig, sig, ACT.Exp, scale=-1.0).then_inc(sig_ready, 1)

                def outputs_read(m):
                    act.wait_ge(pv_done, m * JT + JT)
                    act.wait_ge(var_full, m)
                    act.activation(spread, heads_bank[:], ACT.Copy).then_inc(a_copied, 1)
                    act.wait_ge(gt_split, m)
                    act.activation(norm, sums_bank[:], ACT.Square, scale=EPS ** 0.5).then_inc(sum_squared, 1)

                def squares(m):
                    act.wait_ge(centred, m + 1)
                    act.activation(spread, sums_bank[:], ACT.Square).then_inc(squared, 1)

                def inverse_spread(m):
                    act.wait_ge(var_summed, m + 1)
                    act.activation(norm, norm, ACT.Ln).then_inc(root_ln, 1)
                    act.wait_ge(root_ln, m + 1)
                    act.activation(norm, norm, ACT.Exp, scale=-0.5).then_inc(root_ready, 1)

                def gated_hi(m, et):
                    act.wait_ge(gt_ready, m + 1)
                    act.activation(gth[:, et], norm, ACT.Copy).then_inc(gt_hi, 1)

                def body(b, last=False):
                    for et in range(KT):
                        m = b * KT + et
                        gate_inverse(m)
                        if et:
                            gated_hi(m - 1, et - 1)
                        if et == 2 and not last:
                            inverse_root(b + (NG + 1))
                        outputs_read(m)
                        if et < KT - 1:
                            query(m + 1)
                            squares(m)
                            decays(m + 1, et + 1)
                            key(m + 1)
                            inverse_spread(m)
                            gate_exp(m + 1, et + 1)
                            continue
                        if not last:
                            turned_hi_part(b + 1, 0)
                            turned_hi_part(b + 1, 1)
                        squares(m)
                        if not last:
                            turned_hi_part(b + 1, 2)
                            turned_hi_part(b + 1, 3)
                        inverse_spread(m)
                        gated_hi(m, et)
                        if not last:
                            query(m + 1)
                            decays(m + 1, 0)
                            key(m + 1)
                            gate_exp(m + 1, 0)

                act.wait_ge(biases_ready, 2)
                act.mul(cols[:, 5], cols[:, 2], -1.0).then_inc(cols_ready, 1)
                for j in range(3):
                    weight_hi(j)
                inverse_root(NG)
                for i in range(GT):
                    turned_hi_part(0, i)
                for j in range(3, 5):
                    weight_hi(j)
                act.wait_ge(cols_ready, 1)
                query(0)
                act.wait_ge(small2_in, 16 * 3)
                act.wait_ge(dif_ready, 1)
                decays(0, 0)
                act.wait_ge(kz_zeroed, 2)
                key(0)
                gate_exp(0, 0)
                with act.Fori(0, AG - 1) as b:
                    body(b)
                body(AG - 1, last=True)

            route(0)
            experts(0)
            retention()
            route(1)
            experts(1)

        @block.vector
        def _(dve):
            step = Steps(dve, dve_step)
            dve.wait_ge(biases_turned, 2)
            dve.tensor_copy(cols[:, 0:5].rearrange("p n k -> p (n k)"), out_bank[3][:, 0:5 * KT]).then_inc(biases_ready, 1)
            dve.tensor_copy(b1T[:], out_bank[2][:, 0:NE * HT]).then_inc(biases_ready, 1)
            dve.wait_ge(const_ready, 7)

            def row_stats(loaded):
                for i in range(GT):
                    if loaded:
                        dve.wait_ge(loaded[i][0], loaded[i][1])
                    ins = dve.bn_stats(st6[:, i], xt[:, i])
                step(ins)
                carry_wait(dve)
                for i in range(GT):
                    ins = dve.bn_aggr(mv[:, i], st6[:, i])
                step(ins)
                dve.tensor_scalar(var[:], mv[:, :, 1], EPS, None, ALU.add).then_inc(var_ready, 1)

            def row_norm(ready, free, groups):
                dve.wait_ge(rstd_ready, groups + 1)
                step(dve.tensor_tensor(newton[:], rstd[:], rstd[:], ALU.mult))
                step(dve.tensor_tensor(newton[:], newton[:], var[:], ALU.mult))
                step(dve.tensor_scalar(newton[:], newton[:], -0.5, 1.5, ALU.mult, ALU.add))
                step(dve.tensor_tensor(rstd[:], rstd[:], newton[:], ALU.mult))
                for i in range(GT):
                    if free:
                        dve.wait_ge(free[i][0], free[i][1])
                    dve.tensor_scalar(xn[:, i], xt[:, i], mv[:, i, 0:1], rstd[:, i:i + 1],
                                      ALU.subtract, ALU.mult).then_inc(ready, 1)

            def route(f):
                if f:
                    step(dve.memset(carry[:], 0.0))
                with dve.Fori(0, NG) as g:
                    k = g + f * NG
                    step.loop(g, 29)
                    row_stats([(x_in[i], k * 16 + 16) for i in range(GT)])
                    row_norm(xn_ready, [(scattered[i], k * 32) for i in range(GT)], k + f * AG)
                    dve.wait_ge(logits_full, k * GT + GT)
                    dve.tensor_copy(lg[:].rearrange("p g e -> p (g e)"), out_bank[0][:, 0:GT * NE]).then_inc(logits_copied, 1)
                    dve.wait_ge(logits_copied, k + 1)
                    step(dve.tensor_reduce(mx[:], lg[:], AX_X, ALU.max))
                    dve.tensor_tensor(lg[:], lg[:], mx[:].unsqueeze(2).broadcast_to([P, GT, NE]), ALU.subtract).then_inc(shifted, 1)
                    dve.wait_ge(exp_ready, k + 1)
                    step(dve.tensor_reduce(sm[:], ex[:], AX_X, ALU.add))
                    step(dve.reciprocal(sm[:], sm[:]))
                    ins = (dve.tensor_tensor(gates[:], ex[:], sm[:].unsqueeze(2).broadcast_to([P, GT, NE]), ALU.mult))
                    step(ins)
                    carry_wait(dve)
                    for i in range(GT):
                        ins = dve.max(top[:, i], gates[:, i])
                    step(ins)
                    carry_wait(dve)
                    for i in range(GT):
                        ins = dve.max_index(topi[:, i], top[:, i], gates[:, i])
                    step(ins)
                    step(dve.tensor_copy(topf[:], topi[:, :, 0:2]))
                    step(dve.tensor_tensor(oh[:], iota8[:].unsqueeze(1).unsqueeze(1).broadcast_to([P, GT, 2, NE]),
                                           topf[:].unsqueeze(3).broadcast_to([P, GT, 2, NE]), ALU.is_equal))
                    dve.tensor_tensor(ohs[:], oh[:, :, 0], oh[:, :, 1], ALU.add).then_inc(chosen, 1)
                    step(dve.scalar_tensor_tensor(tsum[:], top[:, :, 0], 1e-8, top[:, :, 1], ALU.add, ALU.add))
                    step(dve.reciprocal(tsum[:], tsum[:]))
                    step(dve.tensor_tensor(wk2[:], top[:, :, 0:2], tsum[:].unsqueeze(2).broadcast_to([P, GT, 2]), ALU.mult))
                    dve.wait_ge(counted, k + 1)
                    step(dve.tensor_tensor(count[:], out_bank[1][:, 0:GT * NE].rearrange("p (g e) -> p g e", g=GT),
                                           carry[:].unsqueeze(1).broadcast_to([P, GT, NE]), ALU.add))
                    step(dve.tensor_tensor(carry[:], carry[:], out_bank[1][:, GT * NE:(GT + 1) * NE], ALU.add), wait=False)
                    step(dve.scalar_tensor_tensor(gslot[:], count[:], float(CAP - 1), slot0[:], ALU.min, ALU.add), wait=False)
                    step(dve.tensor_scalar(sslot[:], count[:], float(CAP), FAR, ALU.is_ge, ALU.mult))
                    step(dve.tensor_tensor(sslot[:], sslot[:], gslot[:], ALU.add))
                    step(dve.tensor_tensor(pick[:], oh[:], sslot[:].unsqueeze(2).broadcast_to([P, GT, 2, NE]), ALU.mult))
                    step(dve.tensor_reduce(scf[:], pick[:], AX_X, ALU.add))
                    dve.tensor_copy(sci[:], scf[:]).then_inc(slots_ready, 1)
                    step(dve.tensor_tensor(pick[:], oh[:], gslot[:].unsqueeze(2).broadcast_to([P, GT, 2, NE]), ALU.mult))
                    step(dve.tensor_reduce(gaf[:], pick[:], AX_X, ALU.add))
                    step(dve.tensor_copy(gidx[:, bass.ds(g * GT, GT), :], gaf[:]), wait=False)
                    step(dve.tensor_scalar(vld[:], scf[:], FAR, 0.5, ALU.is_lt, ALU.mult))
                    step(dve.tensor_tensor(wgt[:, bass.ds(g * GT, GT), :], wk2[:], vld[:], ALU.mult))
                step.end(NG)

            def turn_split(base):
                for s in range(ST):
                    dve.wait_ge(turned_hi, base + (s + 1))
                    dve.tensor_tensor(bTl[:, :, s * P:(s + 1) * P], h_bank[(s + 2) % 3][:].rearrange("p (k t) -> p k t", k=KT),
                                      bTh[:, :, s * P:(s + 1) * P].bitcast(F32), ALU.subtract).then_inc(turned_split, 1)

            def experts(f):
                def body(e, first_weights=False, last=False):
                    ee = e + f * NE

                    def split_w1(c):
                        dve.wait_ge(w1_hi, ee * NC + (c + 1))
                        dve.tensor_tensor(w1l[:, c % SPL], w1raw[:, c % RAW], w1h[:, c % SPL].bitcast(F32),
                                          ALU.subtract).then_inc(w1_split[c % RAW], 1)

                    def split_w2(c):
                        dve.wait_ge(w2_hi, ee * NC + (c + 1))
                        dve.tensor_tensor(w2l[:, c % SPL], w2raw[:, c % RAW], w2h[:, c % SPL].bitcast(F32),
                                          ALU.subtract).then_inc(w2_split[c % RAW], 1)

                    if first_weights:
                        split_w1(0)
                        split_w1(1)
                        split_w2(0)
                        return
                    for n in range(HT):
                        dve.wait_ge(h_hi, ee * HT + (n + 1))
                        dve.tensor_tensor(hl[:, n % 4], hf[:, n % 2], hh[:, n % 4].bitcast(F32), ALU.subtract).then_inc(h_split, 1)
                        if n % 2 == 1:
                            c = n // 2
                            if c + 2 < NC or not last:
                                split_w1(c + 2)
                            if c + 1 < NC or not last:
                                split_w2(c + 1)
                    turn_split(ee * ST + (f * ST + ST))
                    dve.wait_ge(b_done, ee * HT + HT)
                    dve.wait_ge(b2_in, ee * 16 + 16)
                    for s in range(ST):
                        dve.wait_ge(o_stored[s], ee * 16)
                        dve.tensor_tensor(o[:, s], out_bank[s][:], b2t[:], ALU.add).then_inc(o_ready, 1)

                body(0, first_weights=True)
                turn_split(f * ST * (NE + 1))
                with dve.Fori(0, NE - 1) as e:
                    body(e)
                body(NE - 1, last=True)

            def combine(f):
                with dve.Fori(0, NG) as g:
                    k = g + f * NG
                    step.loop(g, GT)
                    for i in range(GT):
                        dve.wait_ge(residual_in[i], k * 16 + 16)
                        t = g * GT + i
                        for c in range(2):
                            dve.wait_ge(gathered[c][i], k * 16 + 16)
                            ins = dve.scalar_tensor_tensor(xt[:, i], ga[:, i, c], wgt[:, bass.ds(t, 1), c],
                                                           xt[:, i], ALU.mult, ALU.add)
                            if c == 0:
                                step(ins)
                        ins.then_inc(y_ready[i], 1)
                step.end(NG)

            def retention():
                def weight_lo(j):
                    dve.wait_ge(aw_hi, j + 1)
                    n = weight_order[j]
                    dve.tensor_tensor(wl[:, n], wraw[:, n], wh[:, n].bitcast(F32), ALU.subtract).then_inc(aw_split, 1)

                def fold(b, c, src):
                    for i in range(GT):
                        if c == 0:
                            dve.wait_ge(residual_in[i], b * 16 + 16)
                        dve.wait_ge(gathered[c][i], b * 16 + 16)
                        ins = dve.scalar_tensor_tensor(xt[:, i], src[i], wgt[:, bass.ds(b * GT + i, 1), c],
                                                       xt[:, i], ALU.mult, ALU.add)
                        ins.then_inc(y_ready[i] if c else folded, 1)
                    if c == 0:
                        dve.wait_ge(folded, (b + 1) * GT)
                    else:
                        for i in range(GT):
                            dve.wait_ge(y_ready[i], b + 1)

                def bank(user, i):
                    return banks[turn_bank(user, i)]

                def turned_lo_part(b, i):
                    dve.wait_ge(aT_hi, b * GT + (i + 1))
                    dve.tensor_tensor(xTl[:, :, i * P:(i + 1) * P], bank("t", i)[:].rearrange("p (k t) -> p k t", k=KT),
                                      xTh[:, :, i * P:(i + 1) * P].bitcast(F32), ALU.subtract).then_inc(aT_split, 1)

                def value(b, i):
                    dve.wait_ge(v_full, b * JT + (i + 1))
                    dve.tensor_tensor(v[:, i], bank("v", i)[:], bvt[:], ALU.add).then_inc(v_ready, 1)

                def query(m, et):
                    dve.wait_ge(k_split, m)
                    dve.wait_ge(q_full, m + 1)
                    dve.tensor_scalar(pf[:], bank("q", et)[:], cols[:, 0, et:et + 1], float(HD) ** -0.5,
                                      ALU.add, ALU.mult).then_inc(q_evac, 1)
                    dve.wait_ge(q_evac, m + 1)
                    dve.wait_ge(q_hi, m + 1)
                    dve.tensor_tensor(ql[:], pf[:], qh[:].bitcast(F32), ALU.subtract).then_inc(q_split, 1)

                def key(m, et):
                    dve.wait_ge(q_split, m + 1)
                    dve.wait_ge(k_full, m + 1)
                    dve.tensor_scalar(pf[:], bank("k", et)[:], cols[:, 1, et:et + 1], None, ALU.add).then_inc(k_evac, 1)
                    dve.wait_ge(k_evac, m + 1)
                    for h in range(HPT):
                        r = slice(h * HD, (h + 1) * HD)
                        dve.wait_ge(k_hi, m * HPT + (h + 1))
                        ins = dve.tensor_tensor(kzl[r, h], pf[r, :], kzh[r, h].bitcast(F32), ALU.subtract)
                    ins.then_inc(k_split, 1)

                def gate_start(m, et):
                    dve.wait_ge(g_exp, m + 1)
                    dve.tensor_scalar(denom, denom, 1.0, 1e38, ALU.add, ALU.min).then_inc(denom_ready, 1)
                    dve.tensor_scalar(gate[:, et % 2], bank("g", et)[:], cols[:, 2, et:et + 1], None, ALU.add).then_inc(g_evac, 1)

                def gate_end(m, et):
                    dve.wait_ge(sig_ready, m + 1)
                    step(dve.tensor_tensor(denom, denom, sig, ALU.mult))
                    step(dve.scalar_tensor_tensor(sig, denom, 2.0, sig, ALU.subtract, ALU.mult))
                    dve.scalar_tensor_tensor(gate[:, et % 2], sig, -1.0, gate[:, et % 2], ALU.mult, ALU.mult).then_inc(gated, 1)

                def variance(m):
                    dve.wait_ge(sum_squared, m + 1)
                    dve.wait_ge(var_full, m + 1)
                    dve.scalar_tensor_tensor(norm, norm, EPS, heads_bank[:], ALU.max, ALU.add).then_inc(var_summed, 1)

                def scale(m, et):
                    dve.wait_ge(root_ready, m + 1)
                    dve.scalar_tensor_tensor(norm, sums_bank[:], cols[:, 3, et:et + 1], norm, ALU.mult, ALU.mult).then_inc(scaled, 1)

                def gated_output(m, et):
                    dve.wait_ge(scaled, m + 1)
                    dve.wait_ge(gated, m + 1)
                    dve.scalar_tensor_tensor(norm, norm, cols[:, 4, et:et + 1], gate[:, et % 2], ALU.add, ALU.mult).then_inc(gt_ready, 1)

                def gated_lo(m, et):
                    dve.wait_ge(gt_hi, m + 1)
                    dve.tensor_tensor(gtl[:, et], norm, gth[:, et].bitcast(F32), ALU.subtract).then_inc(gt_split, 1)

                def body(b, last=False):
                    for et in range(KT):
                        m = b * KT + et
                        dve.wait_ge(d_ready, m + 1)
                        for jt in range(JT):
                            w = S - jt * P
                            dve.wait_ge(pv_done, m * JT + max(jt - 1, 0))
                            for h in range(HPT):
                                dve.wait_ge(s_full, m * (JT * HPT) + (jt * HPT + h + 1))
                                dve.tensor_tensor(sc[jt % 2 * HPT + h][:, 0:w], banks[2 + h][:, 0:w], dcy[:, h, 0:w],
                                                  ALU.mult).then_inc(p_ready, 1)
                            if jt == 0 and et:
                                gate_start(m, et)
                                scale(m - 1, et - 1)
                            elif jt == 1 and et:
                                gated_output(m - 1, et - 1)
                                if et == KT - 1 and not last:
                                    row_norm(axn_ready, None, b + (NG + 1))
                            elif jt == 2:
                                if et:
                                    gated_lo(m - 1, et - 1)
                                gate_end(m, et)
                        if not last:
                            if et < 2:
                                fold(b + 1, et, [xn[:, i] for i in range(GT)])
                            elif et == 2:
                                row_stats(None)
                        if et < KT - 1:
                            query(m + 1, et + 1)
                            key(m + 1, et + 1)
                            variance(m)
                            continue
                        if not last:
                            for i in range(GT):
                                turned_lo_part(b + 1, i)
                        variance(m)
                        if not last:
                            value(b + 1, 0)
                        scale(m, et)
                        gated_output(m, et)
                        if not last:
                            value(b + 1, 1)
                        gated_lo(m, et)
                        if not last:
                            value(b + 1, 2)
                            value(b + 1, 3)
                            query(m + 1, 0)
                            key(m + 1, 0)
                            gate_start(m + 1, 0)
                    for i in range(GT):
                        dve.wait_ge(o_full, b * GT + (i + 1))
                        dve.wait_ge(res_ready, b * GT + (i + 1))
                        dve.tensor_tensor(xt[:, i], bank("o", i)[:], xt[:, i], ALU.add).then_inc(x2_ready, 1)

                for j in range(3):
                    weight_lo(j)
                fold(0, 0, [xn[:, i] for i in range(GT)])
                fold(0, 1, sc)
                row_stats(None)
                row_norm(axn_ready, None, NG)
                dve.wait_ge(small2_in, 16 * 3)
                dve.wait_ge(kz_zeroed, 2)
                for i in range(GT):
                    turned_lo_part(0, i)
                value(0, 0)
                value(0, 1)
                for j in range(3, 5):
                    weight_lo(j)
                value(0, 2)
                value(0, 3)
                query(0, 0)
                key(0, 0)
                gate_start(0, 0)
                with dve.Fori(0, AG - 1) as b:
                    step.loop(b, 14)
                    body(b)
                step.end(AG - 1)
                body(AG - 1, last=True)

            route(0)
            experts(0)
            retention()
            route(1)
            experts(1)
            combine(1)

        @block.tensor
        def _(pe):
            pe.wait_ge(const_ready, 7)
            pe.wait_ge(small_in, 16 * 7)
            pe.transpose(out_bank[2][:, 0:P], b1rows, ident[:]).then_inc(biases_turned, 1)
            pe.transpose(out_bank[3][:, 0:5 * KT], colrows, ident[0:5 * KT, 0:5 * KT]).then_inc(biases_turned, 1)

            def turn(dst, src):
                for k in range(KT):
                    ins = pe.transpose(dst[:, k * P:(k + 1) * P], src[:, k * P:(k + 1) * P], ident[:])
                return ins

            def route(f):
                if f:
                    pe.wait_ge(x2_ready, AG * GT)
                with pe.Fori(0, NG) as g:
                    k = g + f * NG

                    def logits(i):
                        pe.wait_ge(xT_copied, k * GT + (i + 1))
                        if i == 0:
                            pe.wait_ge(logits_copied, k)
                        for kt in range(KT):
                            ins = pe.matmul(out_bank[0][:, i * NE:(i + 1) * NE], xT[:, i, kt, :], gw[:, kt, :],
                                            start=(kt == 0), stop=(kt == KT - 1))
                        ins.then_inc(logits_full, 1)

                    for i in range(GT):
                        pe.wait_ge(xn_ready, k * GT + (i + 1))
                        if i >= 2:
                            pe.wait_ge(xT_copied, k * GT + (i - 1))
                        else:
                            pe.wait_ge(xT_copied, k * GT)
                        turn(h_bank[i % 2], xn[:, i]).then_inc(xT_full, 1)
                        if i:
                            logits(i - 1)
                    logits(GT - 1)
                    pe.wait_ge(chosen, k + 1)
                    for i in range(GT):
                        pe.matmul(out_bank[1][:, i * NE:(i + 1) * NE], upper[:], ohs[:, i], start=True, stop=(i == 0))
                        for j in range(i):
                            pe.matmul(out_bank[1][:, i * NE:(i + 1) * NE], ones_bf[:], ohs[:, j], start=False, stop=(j == i - 1))
                    for j in range(GT):
                        ins = pe.matmul(out_bank[1][:, GT * NE:(GT + 1) * NE], ones_bf[:], ohs[:, j], start=(j == 0), stop=(j == GT - 1))
                    ins.then_inc(counted, 1)

            def experts(f):
                pe.wait_ge(biases_ready, 2)
                pe.wait_ge(xg_in, f * 16 * (NE + 1) + 16)
                t0 = f * ST * (NE + 1)
                for s in range(ST):
                    if s >= 3:
                        pe.wait_ge(turned_split, t0 + s - 2)
                    turn(h_bank[(s + 2) % 3], xg[:, s]).then_inc(turned, 1)
                with pe.Fori(0, NE) as e:
                    ee = e + f * NE
                    turns = ee * ST + (f * ST + ST)

                    def hidden(n):
                        c, j = n // HPC, n % HPC
                        if j == 0:
                            pe.wait_ge(w1_split[c % RAW], ee * (NC // RAW) + (c // RAW + 1))
                        if n == 0:
                            pe.wait_ge(turned_split, turns)
                        for half in range(2):
                            u = 2 * n + half
                            if u >= 3:
                                pe.wait_ge(h_evac, ee * (2 * HT) + (u - 2))
                            r = slice(half * HALF, (half + 1) * HALF)
                            for kt in range(KT):
                                hi, lo = (w[:, c % SPL, kt, j * P:(j + 1) * P] for w in (w1h, w1l))
                                for i, (w, t) in enumerate(((hi, bTh), (hi, bTl), (lo, bTh))):
                                    ins = pe.matmul(h_bank[u % 3][:, 0:HALF], w, t[:, kt, r],
                                                    start=(kt == 0 and i == 0), stop=(kt == KT - 1 and i == 2))
                            ins.then_inc(h_full, 1)
                            last = ins
                        return last

                    def output(n):
                        c, j = n // HPC, n % HPC
                        pe.wait_ge(h_split, ee * HT + (n + 1))
                        if j == 0:
                            pe.wait_ge(w2_split[c % RAW], ee * (NC // RAW) + (c // RAW + 1))
                        if n == 0:
                            pe.wait_ge(o_ready, ee * ST)
                        for s in range(ST):
                            hi, lo = (t[:, n % 4, s * P:(s + 1) * P] for t in (hh, hl))
                            for i, (t, w) in enumerate(((hi, w2h), (hi, w2l), (lo, w2h))):
                                ins = pe.matmul(out_bank[s][:], t, w[:, c % SPL, j, :],
                                                start=(n == 0 and i == 0), stop=(n == HT - 1 and i == 2))
                        ins.then_inc(b_done, 1)

                    def turn_next(s):
                        if s == 0:
                            pe.wait_ge(xg_in, ee * 16 + (f * 16 + 32))
                        if s < 3:
                            pe.wait_ge(h_evac, ee * (2 * HT) + (2 * HT - 2 + s))
                        else:
                            pe.wait_ge(turned_split, turns + (s - 2))
                        turn(h_bank[(s + 2) % 3], xg[:, s]).then_inc(turned, 1)

                    for n in range(HT):
                        hidden(n)
                        if n >= 2:
                            output(n - 2)
                    for s in range(3):
                        turn_next(s)
                    output(HT - 2)
                    for s in range(3, ST):
                        turn_next(s)
                    output(HT - 1)

            def retention():
                def three(dst, pairs):
                    for n, ((sh, sl), (mh, ml)) in enumerate(pairs):
                        first, final = n == 0, n == len(pairs) - 1
                        pe.matmul(dst, sh, mh, start=first, stop=False)
                        pe.matmul(dst, sh, ml, start=False, stop=False)
                        ins = pe.matmul(dst, sl, mh, start=False, stop=final)
                    return ins

                def bank(user, i):
                    return banks[turn_bank(user, i)]

                def project(user, w, et, done):
                    cs = slice(et * P, (et + 1) * P)
                    three(bank(user, et)[:], [((wh[:, w, kt, cs], wl[:, w, kt, cs]), (xTh[:, kt], xTl[:, kt]))
                                              for kt in range(KT)]).then_inc(done, 1)

                def turn_rows(b, i):
                    pe.wait_ge(axn_ready, b * GT + (i + 1))
                    if i >= 2:
                        pe.wait_ge(aT_split, b * GT + (i - 1))
                    turn(bank("t", i), xn[:, i]).then_inc(aT_full, 1)

                def value(b, i):
                    if i < 2:
                        pe.wait_ge(aT_split, b * GT + (i + 3))
                    else:
                        pe.wait_ge(v_ready, b * JT + (i - 1))
                    ts = slice(i * P, (i + 1) * P)
                    three(bank("v", i)[:], [((xTh[:, kt, ts], xTl[:, kt, ts]), (wh[:, WV, kt], wl[:, WV, kt]))
                                            for kt in range(KT)]).then_inc(v_full, 1)

                def first_projections(b, m, weights_first=False):
                    if weights_first:
                        pe.wait_ge(aw_split, 2)
                    pe.wait_ge(v_ready, b * JT + (JT - 1))
                    project("q", WQ, 0, q_full)
                    if weights_first:
                        pe.wait_ge(aw_split, 3)
                    pe.wait_ge(v_ready, b * JT + JT)
                    project("k", WK, 0, k_full)
                    if weights_first:
                        pe.wait_ge(aw_split, 5)
                    pe.wait_ge(q_evac, m + 1)
                    project("g", WG, 0, g_full)

                def centre_heads(m):
                    pe.wait_ge(a_copied, m + 1)
                    pe.wait_ge(sum_squared, m + 1)
                    pe.matmul(sums_bank[:], centre[:], spread, start=True, stop=True).then_inc(centred, 1)

                def head_variance(m):
                    pe.wait_ge(squared, m + 1)
                    pe.matmul(heads_bank[:], headmean[:], spread, start=True, stop=True).then_inc(var_full, 1)

                def scores(m, jt):
                    for h in range(HPT):
                        if jt:
                            pe.wait_ge(p_ready, m * (JT * HPT) + ((jt - 1) * HPT + h + 1))
                        elif h == 0:
                            pe.wait_ge(p_ready, m * (JT * HPT))
                        ks = slice(jt * P, (jt + 1) * P)
                        three(banks[2 + h][:, 0:S - jt * P], [((kzh[:, h, ks], kzl[:, h, ks]), (qh[:, jt * P:S], ql[:, jt * P:S]))]
                              ).then_inc(s_full, 1)

                def values(m, et, jt):
                    if jt == 0:
                        pe.wait_ge(var_summed, m)
                        pe.wait_ge(scaled, m)
                    pe.wait_ge(p_ready, m * (JT * HPT) + (jt + 1) * HPT)
                    for dst, ones in ((heads_bank, False), (sums_bank, True)):
                        for h in range(HPT):
                            hd = et * HPT + h
                            lhsT = ones32[:] if ones else v[:, jt, hd * HD:(hd + 1) * HD]
                            ins = pe.matmul(dst[h * HD:(h + 1) * HD, jt * P:S], lhsT, sc[jt % 2 * HPT + h][:, 0:S - jt * P],
                                            start=(jt == 0), stop=(jt == JT - 1))
                    ins.then_inc(pv_done, 1)

                def body(b, last=False):
                    for et in range(KT):
                        m = b * KT + et
                        pe.wait_ge(q_split, m + 1)
                        pe.wait_ge(k_split, m + 1)
                        if et == 0:
                            pe.wait_ge(v_ready, b * JT + JT)
                        scores(m, 0)
                        for jt in range(1, JT):
                            scores(m, jt)
                            values(m, et, jt - 1)
                        values(m, et, JT - 1)
                        if et < KT - 1:
                            if et == 0:
                                pe.wait_ge(x2_ready, b * GT)
                            pe.wait_ge(k_evac, m + 1)
                            project("q", WQ, et + 1, q_full)
                            centre_heads(m)
                            pe.wait_ge(g_evac, m + 1)
                            project("k", WK, et + 1, k_full)
                            head_variance(m)
                            pe.wait_ge(q_evac, m + 2)
                            project("g", WG, et + 1, g_full)
                            continue
                        if not last:
                            pe.wait_ge(k_evac, m + 1)
                            turn_rows(b + 1, 0)
                            pe.wait_ge(g_evac, m + 1)
                            turn_rows(b + 1, 1)
                        centre_heads(m)
                        if not last:
                            turn_rows(b + 1, 2)
                            turn_rows(b + 1, 3)
                        head_variance(m)
                        if not last:
                            for i in range(JT):
                                value(b + 1, i)
                            first_projections(b + 1, m + 1)
                    m = b * KT + (KT - 1)
                    pe.wait_ge(gt_split, m + 1)
                    for i in range(GT):
                        ts = slice(i * P, (i + 1) * P)
                        if i >= 2:
                            pe.wait_ge(x2_ready, b * GT + (i - 1))
                        elif last:
                            pe.wait_ge(g_evac, m + 1)
                            pe.wait_ge(k_evac, m + 1)
                        elif i == 0:
                            pe.wait_ge(k_evac, m + 2)
                        else:
                            pe.wait_ge(g_evac, m + 2)
                        three(bank("o", i)[:], [((gth[:, kt, ts], gtl[:, kt, ts]), (wh[:, WO, kt], wl[:, WO, kt]))
                                                for kt in range(KT)]).then_inc(o_full, 1)

                pe.wait_ge(o_ready, ST * NE)
                for i in range(GT):
                    turn_rows(0, i)
                pe.wait_ge(aw_split, 1)
                for i in range(JT):
                    value(0, i)
                first_projections(0, 0, weights_first=True)
                with pe.Fori(0, AG - 1) as b:
                    body(b)
                body(AG - 1, last=True)

            route(0)
            experts(0)
            retention()
            route(1)
            experts(1)


_INS = ['L0_attn_x', 'L0_attn_Wq', 'L0_attn_bq', 'L0_attn_Wk', 'L0_attn_bk', 'L0_attn_Wv', 'L0_attn_bv', 'L0_attn_Wg',
        'L0_attn_bg', 'L0_attn_Wo', 'L0_attn_bo', 'L0_attn_gn_w', 'L0_attn_gn_b', 'L0_attn_decay', 'L0_ffn_gating_w',
        'L0_ffn_w1', 'L0_ffn_b1', 'L0_ffn_w2', 'L0_ffn_b2']
_OUTS = [((4, 512, 512), 'float32')]


def kernel(**inputs):
    import numpy as _np
    import concourse.bacc as _bacc
    from concourse import mybir as _mybir
    from concourse.bass_utils import run_bass_kernel_spmd as _run

    nc = _bacc.Bacc("TRN2", target_bir_lowering=False, num_devices=1)
    arrays, args = {}, []
    for name in _INS:
        a = _np.ascontiguousarray(inputs[name])
        arrays[f"in_{name}_dram"] = a
        args.append(nc.dram_tensor(f"in_{name}_dram", a.shape, _mybir.dt.from_np(a.dtype), kind="ExternalInput").ap())
    for i, (shape, dtype) in enumerate(_OUTS):
        dt = _mybir.dt.from_np(_np.dtype(dtype))
        args.append(nc.dram_tensor(f"out_{i}_dram", shape, dt, kind="ExternalOutput").ap())
    macaron_program(nc, *args)
    r = _run(nc, [arrays], core_ids=[0])
    got = tuple(r.results[0][f"out_{i}_dram"] for i in range(len(_OUTS)))
    return got[0]
```
